# Optimizing a Trainium2 kernel written in Bass

```python
import numpy as np
import jax
import jax.numpy as jnp

def _softmax(x, axis=-1):
    return jax.nn.softmax(x, axis=axis)

def _gelu(x):
    return jax.nn.gelu(x, approximate=True)

def _silu(x):
    return jax.nn.silu(x)

def _sigmoid(x):
    return jax.nn.sigmoid(x)

def _layernorm(x, axis=-1, eps=1e-05):
    m = jnp.mean(x, axis=axis, keepdims=True)
    v = jnp.var(x, axis=axis, keepdims=True)
    return (x - m) / jnp.sqrt(v + eps)

def _scatter_add(tgt, idx, src, axis=0):
    return tgt.at[idx].add(src)

def _segment_sum(src, seg, n):
    return jax.ops.segment_sum(src, seg, n)
kernel_name = 'mk_xattn_seq_d4_seqx_r8_f4bdc3'

def setup_inputs(seed: int=0):
    np.random.seed(seed)
    _w = jnp.asarray

    def _rec_inputs():
        import jax
        import jax.numpy as jnp
        _rk = jax.random.key(seed)
        x = -0.000125 + 0.9999 * jax.random.normal(jax.random.fold_in(_rk, 1), (64, 64, 256), jnp.float32)
        _lenS = 64 - jax.random.randint(jax.random.fold_in(_rk, 7), (64,), 0, max(1, 64 // 4) + 1, jnp.int32)
        _lenS2 = 64 - jax.random.randint(jax.random.fold_in(_rk, 8), (64,), 0, max(1, 64 // 4) + 1, jnp.int32)
        _ctx_1024P = jax.random.normal(jax.random.fold_in(_rk, 11), (64, 16, 128), jnp.float32)
        _ctx_1024c = jax.random.dirichlet(jax.random.fold_in(_rk, 511), 0.3 * jnp.ones((16,), jnp.float32), (64, 64))
        _ctx_1024t = jnp.einsum('bsk,bkd->bsd', _ctx_1024c, _ctx_1024P)
        _ctx_1024t = _ctx_1024t * jax.lax.rsqrt(jnp.mean(jnp.square(_ctx_1024t)) + 1e-12) * 0.953939
        ctx_1024 = 4.13588e-05 + 0.999923 * (_ctx_1024t + 0.3 * jax.random.normal(jax.random.fold_in(_rk, 611), (64, 64, 128), jnp.float32))
        pos_1xS = jnp.broadcast_to(jnp.arange(64, dtype=jnp.int32), (1, 64))
        _validS = jnp.arange(64)[None, :] < _lenS[:, None]
        _validS2 = jnp.arange(64)[None, :] < _lenS2[:, None]
        _causal = jnp.tril(jnp.ones((64, 64), dtype=bool))
        mask_BxS2_bk0 = jnp.logical_not(jnp.broadcast_to(_validS2[:, :], (64, 64)))
        mask_BxS_ik0 = jnp.where(jnp.broadcast_to(_validS[:, :], (64, 64)), 0, 1).astype(jnp.int32)
        return (x, ctx_1024, pos_1xS, mask_BxS2_bk0, mask_BxS_ik0)
    x, ctx_1024, pos_1xS, mask_BxS2_bk0, mask_BxS_ik0 = _rec_inputs()

    def _L0_xattn_setup():
        import jax, jax.numpy as jnp
        import numpy as np
        EPS = 1e-06

        def _rmsnorm(x, w):
            var = jnp.mean(jnp.square(x), axis=-1, keepdims=True)
            return x * jax.lax.rsqrt(var + EPS) * w
        key = jax.random.key(seed)
        ks = jax.random.split(key, 6)
        B, N, M = (4, 512, 256)
        d_model, memory_dim = (256, 128)
        hidden_states = jax.random.normal(ks[0], (B, N, d_model), dtype=jnp.float32)
        memory = jax.random.normal(ks[1], (B, M, memory_dim), dtype=jnp.float32)
        W_mem = jax.random.normal(ks[2], (d_model, memory_dim), dtype=jnp.float32) / np.sqrt(memory_dim)
        W_gate = jax.random.normal(ks[3], (d_model, 2 * d_model), dtype=jnp.float32) / np.sqrt(2 * d_model)
        b_gate = jax.random.normal(ks[4], (d_model,), dtype=jnp.float32) * 0.01
        norm_w = jnp.ones((d_model,), dtype=jnp.float32)
        return {'hidden_states': hidden_states, 'memory': memory, 'W_mem': W_mem, 'W_gate': W_gate, 'b_gate': b_gate, 'norm_w': norm_w}
    _L0_xattn_all = _L0_xattn_setup()
    _L0_xattn_in = {k: v for k, v in _L0_xattn_all.items() if k in ('W_mem', 'W_gate', 'b_gate', 'norm_w')}
    del _L0_xattn_all

    def _L1_xattn_setup():
        import jax, jax.numpy as jnp
        import numpy as np
        DIM = 256
        DIM_MEDIA = 128
        HEADS = 16
        DIM_HEAD = 64
        INNER = HEADS * DIM_HEAD
        FF_INNER = 4 * DIM
        B, N_TOK, N_LAT = (4, 256, 64)
        EPS = 1e-05

        def layernorm(x, g, b):
            mu = jnp.mean(x, axis=-1, keepdims=True)
            var = jnp.var(x, axis=-1, keepdims=True)
            return (x - mu) * jax.lax.rsqrt(var + EPS) * g + b
        key = jax.random.key(seed)
        ks = jax.random.split(key, 12)
        x = jax.random.normal(ks[0], (B, N_TOK, DIM), dtype=jnp.float32)
        media = jax.random.normal(ks[1], (B, N_LAT, DIM_MEDIA), dtype=jnp.float32)
        media_mask = jax.random.randint(ks[2], (B, N_LAT), 0, 2).astype(bool)
        media_mask = media_mask.at[:, 0].set(True)
        s = lambda d: 1.0 / np.sqrt(d)
        Wq = jax.random.normal(ks[3], (DIM, INNER), dtype=jnp.float32) * s(DIM)
        Wkv = jax.random.normal(ks[4], (DIM_MEDIA, 2 * INNER), dtype=jnp.float32) * s(DIM_MEDIA)
        Wo = jax.random.normal(ks[5], (INNER, DIM), dtype=jnp.float32) * s(INNER)
        W1 = jax.random.normal(ks[6], (DIM, FF_INNER), dtype=jnp.float32) * s(DIM)
        W2 = jax.random.normal(ks[7], (FF_INNER, DIM), dtype=jnp.float32) * s(FF_INNER)
        return {'x': x, 'media': media, 'media_mask': media_mask, 'ln_q_g': jnp.ones((DIM,), jnp.float32), 'ln_q_b': jnp.zeros((DIM,), jnp.float32), 'Wq': Wq, 'Wkv': Wkv, 'Wo': Wo, 'attn_gate': jax.random.normal(ks[8], (1,), jnp.float32) * 0.5, 'ln_ff_g': jnp.ones((DIM,), jnp.float32), 'ln_ff_b': jnp.zeros((DIM,), jnp.float32), 'W1': W1, 'W2': W2, 'ff_gate': jax.random.normal(ks[9], (1,), jnp.float32) * 0.5}
    _L1_xattn_all = _L1_xattn_setup()
    _L1_xattn_in = {k: v for k, v in _L1_xattn_all.items() if k in ('ln_q_g', 'ln_q_b', 'Wq', 'Wkv', 'Wo', 'attn_gate', 'ln_ff_g', 'ln_ff_b', 'W1', 'W2', 'ff_gate')}
    del _L1_xattn_all

    def _L2_xattn_setup():
        import jax, jax.numpy as jnp
        import numpy as np
        H = 256
        NH = 16
        HD = H // NH
        CH = 128
        CC = 128
        CHD = CC // NH
        I = 688
        B = 2
        L = 256
        LE = 128
        EPS = 1e-06

        def rms_norm(x, w):
            xf = x.astype(jnp.float32)
            var = jnp.mean(xf * xf, axis=-1, keepdims=True)
            return (w * (xf * jax.lax.rsqrt(var + EPS))).astype(x.dtype)

        def expert_mask(tt):
            vm = jnp.zeros(tt.shape, dtype=bool)
            vm = vm.at[:, :-1].set((tt[:, :-1] == 1) & (tt[:, 1:] == 1))
            return vm

        def rotate_half(x):
            d = x.shape[-1] // 2
            return jnp.concatenate([-x[..., d:], x[..., :d]], axis=-1)

        def apply_rotary(q, k, position_ids, seq_len):
            inv = 1.0 / 10000.0 ** (jnp.arange(0, HD, 2, dtype=jnp.float32) / HD)
            t = jnp.arange(seq_len, dtype=jnp.float32)
            freqs = jnp.outer(t, inv)
            emb = jnp.concatenate([freqs, freqs], axis=-1)
            cos = jnp.cos(emb)[position_ids][:, None].astype(q.dtype)
            sin = jnp.sin(emb)[position_ids][:, None].astype(q.dtype)
            return (q * cos + rotate_half(q) * sin, k * cos + rotate_half(k) * sin)

        def sdpa(q, k, v, causal):
            scale = 1.0 / np.sqrt(q.shape[-1])
            scores = jnp.einsum('bhqd,bhkd->bhqk', q * scale, k)
            if causal:
                mask = jnp.tril(jnp.ones((q.shape[-2], k.shape[-2]), dtype=bool))
                scores = jnp.where(mask, scores, jnp.finfo(jnp.float32).min)
            p = jax.nn.softmax(scores.astype(jnp.float32), axis=-1).astype(q.dtype)
            return jnp.einsum('bhqk,bhkd->bhqd', p, v)

        def heads(x, nh, hd):
            b, l, _ = x.shape
            return x.reshape(b, l, nh, hd).transpose(0, 2, 1, 3)
        key = jax.random.key(seed)
        ks = jax.random.split(key, 20)
        s = 0.02
        f32 = jnp.float32
        return {'hidden_states': jax.random.normal(ks[0], (B, L, H), f32), 'encoder_outputs': jax.random.normal(ks[1], (B, LE, CH), f32), 'token_type_ids': jax.random.randint(ks[2], (B, L), 0, 2, jnp.int32), 'position_ids': jnp.arange(L, dtype=jnp.int32)[None, :], 'ln_in_w': jnp.ones((H,), f32), 'ln_post_attn_w': jnp.ones((H,), f32), 'ln_post_cross_w': jnp.ones((H,), f32), 'v_qkv': jax.random.normal(ks[3], (H, 3 * H), f32) * s, 'l_qkv': jax.random.normal(ks[4], (H, 3 * H), f32) * s, 'v_dense': jax.random.normal(ks[5], (H, H), f32) * s, 'l_dense': jax.random.normal(ks[6], (H, H), f32) * s, 'cq_w': jax.random.normal(ks[7], (H, CC), f32) * s, 'ckv_w': jax.random.normal(ks[8], (CH, 2 * CC), f32) * s, 'cdense_w': jax.random.normal(ks[9], (CC, H), f32) * s, 'v_gate': jax.random.normal(ks[10], (H, I), f32) * s, 'v_up': jax.random.normal(ks[11], (H, I), f32) * s, 'v_down': jax.random.normal(ks[12], (I, H), f32) * s, 'l_gate': jax.random.normal(ks[13], (H, I), f32) * s, 'l_up': jax.random.normal(ks[14], (H, I), f32) * s, 'l_down': jax.random.normal(ks[15], (I, H), f32) * s}
    _L2_xattn_all = _L2_xattn_setup()
    _L2_xattn_in = {k: v for k, v in _L2_xattn_all.items() if k in ('ln_in_w', 'ln_post_attn_w', 'ln_post_cross_w', 'v_qkv', 'l_qkv', 'v_dense', 'l_dense', 'cq_w', 'ckv_w', 'cdense_w', 'v_gate', 'v_up', 'v_down', 'l_gate', 'l_up', 'l_down')}
    del _L2_xattn_all

    def _L3_xattn_setup():
        import jax, jax.numpy as jnp
        import numpy as np
        H = 256
        NH = 16
        HD = H // NH
        CH = 128
        CC = 128
        CHD = CC // NH
        I = 688
        B = 2
        L = 256
        LE = 128
        EPS = 1e-06

        def rms_norm(x, w):
            xf = x.astype(jnp.float32)
            var = jnp.mean(xf * xf, axis=-1, keepdims=True)
            return (w * (xf * jax.lax.rsqrt(var + EPS))).astype(x.dtype)

        def expert_mask(tt):
            vm = jnp.zeros(tt.shape, dtype=bool)
            vm = vm.at[:, :-1].set((tt[:, :-1] == 1) & (tt[:, 1:] == 1))
            return vm

        def rotate_half(x):
            d = x.shape[-1] // 2
            return jnp.concatenate([-x[..., d:], x[..., :d]], axis=-1)

        def apply_rotary(q, k, position_ids, seq_len):
            inv = 1.0 / 10000.0 ** (jnp.arange(0, HD, 2, dtype=jnp.float32) / HD)
            t = jnp.arange(seq_len, dtype=jnp.float32)
            freqs = jnp.outer(t, inv)
            emb = jnp.concatenate([freqs, freqs], axis=-1)
            cos = jnp.cos(emb)[position_ids][:, None].astype(q.dtype)
            sin = jnp.sin(emb)[position_ids][:, None].astype(q.dtype)
            return (q * cos + rotate_half(q) * sin, k * cos + rotate_half(k) * sin)

        def sdpa(q, k, v, causal):
            scale = 1.0 / np.sqrt(q.shape[-1])
            scores = jnp.einsum('bhqd,bhkd->bhqk', q * scale, k)
            if causal:
                mask = jnp.tril(jnp.ones((q.shape[-2], k.shape[-2]), dtype=bool))
                scores = jnp.where(mask, scores, jnp.finfo(jnp.float32).min)
            p = jax.nn.softmax(scores.astype(jnp.float32), axis=-1).astype(q.dtype)
            return jnp.einsum('bhqk,bhkd->bhqd', p, v)

        def heads(x, nh, hd):
            b, l, _ = x.shape
            return x.reshape(b, l, nh, hd).transpose(0, 2, 1, 3)
        key = jax.random.key(seed)
        ks = jax.random.split(key, 20)
        s = 0.02
        f32 = jnp.float32
        return {'hidden_states': jax.random.normal(ks[0], (B, L, H), f32), 'encoder_outputs': jax.random.normal(ks[1], (B, LE, CH), f32), 'token_type_ids': jax.random.randint(ks[2], (B, L), 0, 2, jnp.int32), 'position_ids': jnp.arange(L, dtype=jnp.int32)[None, :], 'ln_in_w': jnp.ones((H,), f32), 'ln_post_attn_w': jnp.ones((H,), f32), 'ln_post_cross_w': jnp.ones((H,), f32), 'v_qkv': jax.random.normal(ks[3], (H, 3 * H), f32) * s, 'l_qkv': jax.random.normal(ks[4], (H, 3 * H), f32) * s, 'v_dense': jax.random.normal(ks[5], (H, H), f32) * s, 'l_dense': jax.random.normal(ks[6], (H, H), f32) * s, 'cq_w': jax.random.normal(ks[7], (H, CC), f32) * s, 'ckv_w': jax.random.normal(ks[8], (CH, 2 * CC), f32) * s, 'cdense_w': jax.random.normal(ks[9], (CC, H), f32) * s, 'v_gate': jax.random.normal(ks[10], (H, I), f32) * s, 'v_up': jax.random.normal(ks[11], (H, I), f32) * s, 'v_down': jax.random.normal(ks[12], (I, H), f32) * s, 'l_gate': jax.random.normal(ks[13], (H, I), f32) * s, 'l_up': jax.random.normal(ks[14], (H, I), f32) * s, 'l_down': jax.random.normal(ks[15], (I, H), f32) * s}
    _L3_xattn_all = _L3_xattn_setup()
    _L3_xattn_in = {k: v for k, v in _L3_xattn_all.items() if k in ('ln_in_w', 'ln_post_attn_w', 'ln_post_cross_w', 'v_qkv', 'l_qkv', 'v_dense', 'l_dense', 'cq_w', 'ckv_w', 'cdense_w', 'v_gate', 'v_up', 'v_down', 'l_gate', 'l_up', 'l_down')}
    del _L3_xattn_all
    return {'x': x, 'ctx_1024': ctx_1024, 'pos_1xS': pos_1xS, 'mask_BxS2_bk0': mask_BxS2_bk0, 'mask_BxS_ik0': mask_BxS_ik0, 'L0_xattn_W_mem': _L0_xattn_in['W_mem'], 'L0_xattn_W_gate': _L0_xattn_in['W_gate'], 'L0_xattn_b_gate': _L0_xattn_in['b_gate'], 'L0_xattn_norm_w': _L0_xattn_in['norm_w'], 'L1_xattn_ln_q_g': _L1_xattn_in['ln_q_g'], 'L1_xattn_ln_q_b': _L1_xattn_in['ln_q_b'], 'L1_xattn_Wq': _L1_xattn_in['Wq'], 'L1_xattn_Wkv': _L1_xattn_in['Wkv'], 'L1_xattn_Wo': _L1_xattn_in['Wo'], 'L1_xattn_attn_gate': _L1_xattn_in['attn_gate'], 'L1_xattn_ln_ff_g': _L1_xattn_in['ln_ff_g'], 'L1_xattn_ln_ff_b': _L1_xattn_in['ln_ff_b'], 'L1_xattn_W1': _L1_xattn_in['W1'], 'L1_xattn_W2': _L1_xattn_in['W2'], 'L1_xattn_ff_gate': _L1_xattn_in['ff_gate'], 'L2_xattn_ln_in_w': _L2_xattn_in['ln_in_w'], 'L2_xattn_ln_post_attn_w': _L2_xattn_in['ln_post_attn_w'], 'L2_xattn_ln_post_cross_w': _L2_xattn_in['ln_post_cross_w'], 'L2_xattn_v_qkv': _L2_xattn_in['v_qkv'], 'L2_xattn_l_qkv': _L2_xattn_in['l_qkv'], 'L2_xattn_v_dense': _L2_xattn_in['v_dense'], 'L2_xattn_l_dense': _L2_xattn_in['l_dense'], 'L2_xattn_cq_w': _L2_xattn_in['cq_w'], 'L2_xattn_ckv_w': _L2_xattn_in['ckv_w'], 'L2_xattn_cdense_w': _L2_xattn_in['cdense_w'], 'L2_xattn_v_gate': _L2_xattn_in['v_gate'], 'L2_xattn_v_up': _L2_xattn_in['v_up'], 'L2_xattn_v_down': _L2_xattn_in['v_down'], 'L2_xattn_l_gate': _L2_xattn_in['l_gate'], 'L2_xattn_l_up': _L2_xattn_in['l_up'], 'L2_xattn_l_down': _L2_xattn_in['l_down'], 'L3_xattn_ln_in_w': _L3_xattn_in['ln_in_w'], 'L3_xattn_ln_post_attn_w': _L3_xattn_in['ln_post_attn_w'], 'L3_xattn_ln_post_cross_w': _L3_xattn_in['ln_post_cross_w'], 'L3_xattn_v_qkv': _L3_xattn_in['v_qkv'], 'L3_xattn_l_qkv': _L3_xattn_in['l_qkv'], 'L3_xattn_v_dense': _L3_xattn_in['v_dense'], 'L3_xattn_l_dense': _L3_xattn_in['l_dense'], 'L3_xattn_cq_w': _L3_xattn_in['cq_w'], 'L3_xattn_ckv_w': _L3_xattn_in['ckv_w'], 'L3_xattn_cdense_w': _L3_xattn_in['cdense_w'], 'L3_xattn_v_gate': _L3_xattn_in['v_gate'], 'L3_xattn_v_up': _L3_xattn_in['v_up'], 'L3_xattn_v_down': _L3_xattn_in['v_down'], 'L3_xattn_l_gate': _L3_xattn_in['l_gate'], 'L3_xattn_l_up': _L3_xattn_in['l_up'], 'L3_xattn_l_down': _L3_xattn_in['l_down']}

def reference(x, ctx_1024, pos_1xS, mask_BxS2_bk0, mask_BxS_ik0, L0_xattn_W_mem, L0_xattn_W_gate, L0_xattn_b_gate, L0_xattn_norm_w, L1_xattn_ln_q_g, L1_xattn_ln_q_b, L1_xattn_Wq, L1_xattn_Wkv, L1_xattn_Wo, L1_xattn_attn_gate, L1_xattn_ln_ff_g, L1_xattn_ln_ff_b, L1_xattn_W1, L1_xattn_W2, L1_xattn_ff_gate, L2_xattn_ln_in_w, L2_xattn_ln_post_attn_w, L2_xattn_ln_post_cross_w, L2_xattn_v_qkv, L2_xattn_l_qkv, L2_xattn_v_dense, L2_xattn_l_dense, L2_xattn_cq_w, L2_xattn_ckv_w, L2_xattn_cdense_w, L2_xattn_v_gate, L2_xattn_v_up, L2_xattn_v_down, L2_xattn_l_gate, L2_xattn_l_up, L2_xattn_l_down, L3_xattn_ln_in_w, L3_xattn_ln_post_attn_w, L3_xattn_ln_post_cross_w, L3_xattn_v_qkv, L3_xattn_l_qkv, L3_xattn_v_dense, L3_xattn_l_dense, L3_xattn_cq_w, L3_xattn_ckv_w, L3_xattn_cdense_w, L3_xattn_v_gate, L3_xattn_v_up, L3_xattn_v_down, L3_xattn_l_gate, L3_xattn_l_up, L3_xattn_l_down):
    import jax
    import jax.numpy as jnp

    def _L0_xattn_ref(hidden_states, memory, W_mem, W_gate, b_gate, norm_w):
        import jax, jax.numpy as jnp
        import numpy as np
        EPS = 1e-06

        def _rmsnorm(x, w):
            var = jnp.mean(jnp.square(x), axis=-1, keepdims=True)
            return x * jax.lax.rsqrt(var + EPS) * w
        D = hidden_states.shape[-1]
        memory_proj = jnp.einsum('bme,de->bmd', memory, W_mem)
        scores = jnp.einsum('bnd,bmd->bnm', hidden_states, memory_proj) / jnp.sqrt(jnp.float32(D))
        attn = jax.nn.softmax(scores, axis=-1)
        memory_context = jnp.einsum('bnm,bmd->bnd', attn, memory_proj)
        gate_input = jnp.concatenate([hidden_states, memory_context], axis=-1)
        gate = jax.nn.sigmoid(jnp.einsum('bnf,df->bnd', gate_input, W_gate) + b_gate)
        fused = hidden_states + gate * memory_context
        return _rmsnorm(fused, norm_w)

    def _L1_xattn_ref(x, media, media_mask, ln_q_g, ln_q_b, Wq, Wkv, Wo, attn_gate, ln_ff_g, ln_ff_b, W1, W2, ff_gate):
        import jax, jax.numpy as jnp
        import numpy as np
        DIM = 256
        DIM_MEDIA = 128
        HEADS = 16
        DIM_HEAD = 64
        INNER = HEADS * DIM_HEAD
        FF_INNER = 4 * DIM
        B, N_TOK, N_LAT = (4, 256, 64)
        EPS = 1e-05

        def layernorm(x, g, b):
            mu = jnp.mean(x, axis=-1, keepdims=True)
            var = jnp.var(x, axis=-1, keepdims=True)
            return (x - mu) * jax.lax.rsqrt(var + EPS) * g + b
        scale = DIM_HEAD ** (-0.5)
        qn = layernorm(x, ln_q_g, ln_q_b)
        q = qn @ Wq * scale
        kv = media @ Wkv
        k, v = jnp.split(kv, 2, axis=-1)
        split_heads = lambda t: t.reshape(t.shape[0], t.shape[1], HEADS, DIM_HEAD).transpose(0, 2, 1, 3)
        q, k, v = (split_heads(q), split_heads(k), split_heads(v))
        sim = jnp.einsum('bhid,bhjd->bhij', q, k)
        neg_inf = jnp.finfo(sim.dtype).min
        sim = jnp.where(media_mask[:, None, None, :], sim, neg_inf)
        attn = jax.nn.softmax(sim, axis=-1)
        out = jnp.einsum('bhij,bhjd->bhid', attn, v)
        out = out.transpose(0, 2, 1, 3).reshape(x.shape[0], x.shape[1], INNER)
        attn_out = out @ Wo
        x = x + jnp.tanh(attn_gate) * attn_out
        h = layernorm(x, ln_ff_g, ln_ff_b)
        h = jax.nn.gelu(h @ W1, approximate=False) @ W2
        x = x + jnp.tanh(ff_gate) * h
        return x

    def _L2_xattn_ref(hidden_states, encoder_outputs, token_type_ids, position_ids, ln_in_w, ln_post_attn_w, ln_post_cross_w, v_qkv, l_qkv, v_dense, l_dense, cq_w, ckv_w, cdense_w, v_gate, v_up, v_down, l_gate, l_up, l_down):
        import jax, jax.numpy as jnp
        import numpy as np
        H = 256
        NH = 16
        HD = H // NH
        CH = 128
        CC = 128
        CHD = CC // NH
        I = 688
        B = 2
        L = 256
        LE = 128
        EPS = 1e-06

        def rms_norm(x, w):
            xf = x.astype(jnp.float32)
            var = jnp.mean(xf * xf, axis=-1, keepdims=True)
            return (w * (xf * jax.lax.rsqrt(var + EPS))).astype(x.dtype)

        def expert_mask(tt):
            vm = jnp.zeros(tt.shape, dtype=bool)
            vm = vm.at[:, :-1].set((tt[:, :-1] == 1) & (tt[:, 1:] == 1))
            return vm

        def rotate_half(x):
            d = x.shape[-1] // 2
            return jnp.concatenate([-x[..., d:], x[..., :d]], axis=-1)

        def apply_rotary(q, k, position_ids, seq_len):
            inv = 1.0 / 10000.0 ** (jnp.arange(0, HD, 2, dtype=jnp.float32) / HD)
            t = jnp.arange(seq_len, dtype=jnp.float32)
            freqs = jnp.outer(t, inv)
            emb = jnp.concatenate([freqs, freqs], axis=-1)
            cos = jnp.cos(emb)[position_ids][:, None].astype(q.dtype)
            sin = jnp.sin(emb)[position_ids][:, None].astype(q.dtype)
            return (q * cos + rotate_half(q) * sin, k * cos + rotate_half(k) * sin)

        def sdpa(q, k, v, causal):
            scale = 1.0 / np.sqrt(q.shape[-1])
            scores = jnp.einsum('bhqd,bhkd->bhqk', q * scale, k)
            if causal:
                mask = jnp.tril(jnp.ones((q.shape[-2], k.shape[-2]), dtype=bool))
                scores = jnp.where(mask, scores, jnp.finfo(jnp.float32).min)
            p = jax.nn.softmax(scores.astype(jnp.float32), axis=-1).astype(q.dtype)
            return jnp.einsum('bhqk,bhkd->bhqd', p, v)

        def heads(x, nh, hd):
            b, l, _ = x.shape
            return x.reshape(b, l, nh, hd).transpose(0, 2, 1, 3)
        b, l, _ = hidden_states.shape
        vm = expert_mask(token_type_ids)[..., None]
        residual = hidden_states
        x = rms_norm(hidden_states, ln_in_w)
        mixed = jnp.where(vm, x @ v_qkv, x @ l_qkv)
        q, k, v = jnp.split(mixed, 3, axis=-1)
        q, k, v = (heads(q, NH, HD), heads(k, NH, HD), heads(v, NH, HD))
        q, k = apply_rotary(q, k, position_ids, l)
        ctx = sdpa(q, k, v, causal=True)
        ctx = ctx.transpose(0, 2, 1, 3).reshape(b, l, H)
        attn_out = jnp.where(vm, ctx @ v_dense, ctx @ l_dense)
        hidden_states = residual + attn_out
        ci = rms_norm(hidden_states, ln_post_cross_w)
        cq = heads(ci @ cq_w, NH, CHD)
        ckv = encoder_outputs @ ckv_w
        ck, cv = jnp.split(ckv, 2, axis=-1)
        ck, cv = (heads(ck, NH, CHD), heads(cv, NH, CHD))
        cctx = sdpa(cq, ck, cv, causal=False)
        cctx = cctx.transpose(0, 2, 1, 3).reshape(b, l, CC)
        hidden_states = hidden_states + cctx @ cdense_w
        mi = rms_norm(hidden_states, ln_post_attn_w)
        v_out = jax.nn.silu(mi @ v_gate) * (mi @ v_up) @ v_down
        l_out = jax.nn.silu(mi @ l_gate) * (mi @ l_up) @ l_down
        hidden_states = hidden_states + jnp.where(vm, v_out, l_out)
        return hidden_states

    def _L3_xattn_ref(hidden_states, encoder_outputs, token_type_ids, position_ids, ln_in_w, ln_post_attn_w, ln_post_cross_w, v_qkv, l_qkv, v_dense, l_dense, cq_w, ckv_w, cdense_w, v_gate, v_up, v_down, l_gate, l_up, l_down):
        import jax, jax.numpy as jnp
        import numpy as np
        H = 256
        NH = 16
        HD = H // NH
        CH = 128
        CC = 128
        CHD = CC // NH
        I = 688
        B = 2
        L = 256
        LE = 128
        EPS = 1e-06

        def rms_norm(x, w):
            xf = x.astype(jnp.float32)
            var = jnp.mean(xf * xf, axis=-1, keepdims=True)
            return (w * (xf * jax.lax.rsqrt(var + EPS))).astype(x.dtype)

        def expert_mask(tt):
            vm = jnp.zeros(tt.shape, dtype=bool)
            vm = vm.at[:, :-1].set((tt[:, :-1] == 1) & (tt[:, 1:] == 1))
            return vm

        def rotate_half(x):
            d = x.shape[-1] // 2
            return jnp.concatenate([-x[..., d:], x[..., :d]], axis=-1)

        def apply_rotary(q, k, position_ids, seq_len):
            inv = 1.0 / 10000.0 ** (jnp.arange(0, HD, 2, dtype=jnp.float32) / HD)
            t = jnp.arange(seq_len, dtype=jnp.float32)
            freqs = jnp.outer(t, inv)
            emb = jnp.concatenate([freqs, freqs], axis=-1)
            cos = jnp.cos(emb)[position_ids][:, None].astype(q.dtype)
            sin = jnp.sin(emb)[position_ids][:, None].astype(q.dtype)
            return (q * cos + rotate_half(q) * sin, k * cos + rotate_half(k) * sin)

        def sdpa(q, k, v, causal):
            scale = 1.0 / np.sqrt(q.shape[-1])
            scores = jnp.einsum('bhqd,bhkd->bhqk', q * scale, k)
            if causal:
                mask = jnp.tril(jnp.ones((q.shape[-2], k.shape[-2]), dtype=bool))
                scores = jnp.where(mask, scores, jnp.finfo(jnp.float32).min)
            p = jax.nn.softmax(scores.astype(jnp.float32), axis=-1).astype(q.dtype)
            return jnp.einsum('bhqk,bhkd->bhqd', p, v)

        def heads(x, nh, hd):
            b, l, _ = x.shape
            return x.reshape(b, l, nh, hd).transpose(0, 2, 1, 3)
        b, l, _ = hidden_states.shape
        vm = expert_mask(token_type_ids)[..., None]
        residual = hidden_states
        x = rms_norm(hidden_states, ln_in_w)
        mixed = jnp.where(vm, x @ v_qkv, x @ l_qkv)
        q, k, v = jnp.split(mixed, 3, axis=-1)
        q, k, v = (heads(q, NH, HD), heads(k, NH, HD), heads(v, NH, HD))
        q, k = apply_rotary(q, k, position_ids, l)
        ctx = sdpa(q, k, v, causal=True)
        ctx = ctx.transpose(0, 2, 1, 3).reshape(b, l, H)
        attn_out = jnp.where(vm, ctx @ v_dense, ctx @ l_dense)
        hidden_states = residual + attn_out
        ci = rms_norm(hidden_states, ln_post_cross_w)
        cq = heads(ci @ cq_w, NH, CHD)
        ckv = encoder_outputs @ ckv_w
        ck, cv = jnp.split(ckv, 2, axis=-1)
        ck, cv = (heads(ck, NH, CHD), heads(cv, NH, CHD))
        cctx = sdpa(cq, ck, cv, causal=False)
        cctx = cctx.transpose(0, 2, 1, 3).reshape(b, l, CC)
        hidden_states = hidden_states + cctx @ cdense_w
        mi = rms_norm(hidden_states, ln_post_attn_w)
        v_out = jax.nn.silu(mi @ v_gate) * (mi @ v_up) @ v_down
        l_out = jax.nn.silu(mi @ l_gate) * (mi @ l_up) @ l_down
        hidden_states = hidden_states + jnp.where(vm, v_out, l_out)
        return hidden_states
    x = _L0_xattn_ref(x, ctx_1024, L0_xattn_W_mem, L0_xattn_W_gate, L0_xattn_b_gate, L0_xattn_norm_w)
    x = _L1_xattn_ref(x, ctx_1024, mask_BxS2_bk0, L1_xattn_ln_q_g, L1_xattn_ln_q_b, L1_xattn_Wq, L1_xattn_Wkv, L1_xattn_Wo, L1_xattn_attn_gate, L1_xattn_ln_ff_g, L1_xattn_ln_ff_b, L1_xattn_W1, L1_xattn_W2, L1_xattn_ff_gate)
    x = _L2_xattn_ref(x, ctx_1024, mask_BxS_ik0, pos_1xS, L2_xattn_ln_in_w, L2_xattn_ln_post_attn_w, L2_xattn_ln_post_cross_w, L2_xattn_v_qkv, L2_xattn_l_qkv, L2_xattn_v_dense, L2_xattn_l_dense, L2_xattn_cq_w, L2_xattn_ckv_w, L2_xattn_cdense_w, L2_xattn_v_gate, L2_xattn_v_up, L2_xattn_v_down, L2_xattn_l_gate, L2_xattn_l_up, L2_xattn_l_down)
    x = _L3_xattn_ref(x, ctx_1024, mask_BxS_ik0, pos_1xS, L3_xattn_ln_in_w, L3_xattn_ln_post_attn_w, L3_xattn_ln_post_cross_w, L3_xattn_v_qkv, L3_xattn_l_qkv, L3_xattn_v_dense, L3_xattn_l_dense, L3_xattn_cq_w, L3_xattn_ckv_w, L3_xattn_cdense_w, L3_xattn_v_gate, L3_xattn_v_up, L3_xattn_v_down, L3_xattn_l_gate, L3_xattn_l_up, L3_xattn_l_down)
    return x

_drawn_inputs = setup_inputs


def setup_inputs(seed=0):
    import zlib

    import numpy as np

    out = dict(_drawn_inputs(seed))
    spreads = {'L0_xattn_norm_w': (1.0, 0.2),
     'L1_xattn_ln_q_g': (1.0, 0.6),
     'L1_xattn_ln_q_b': (0.0, 0.8),
     'L1_xattn_ln_ff_g': (1.0, 0.6),
     'L1_xattn_ln_ff_b': (0.0, 0.8),
     'L2_xattn_ln_in_w': (1.0, 0.6),
     'L2_xattn_ln_post_attn_w': (1.0, 0.6),
     'L2_xattn_ln_post_cross_w': (1.0, 0.6),
     'L3_xattn_ln_in_w': (1.0, 0.6),
     'L3_xattn_ln_post_attn_w': (1.0, 0.6),
     'L3_xattn_ln_post_cross_w': (1.0, 0.6)}
    factors = {'L0_xattn_b_gate': 8.0,
     'L1_xattn_W1': 2.753,
     'L2_xattn_v_qkv': 8.0,
     'L2_xattn_v_dense': 5.819,
     'L2_xattn_cq_w': 64.0,
     'L2_xattn_v_gate': 6.283,
     'L2_xattn_v_up': 6.202,
     'L2_xattn_v_down': 6.228,
     'L3_xattn_v_qkv': 8.0,
     'L3_xattn_v_dense': 5.766,
     'L3_xattn_cq_w': 64.0,
     'L3_xattn_v_gate': 6.552,
     'L3_xattn_v_up': 6.452,
     'L3_xattn_v_down': 6.483,
     'L2_xattn_l_dense': 8.0,
     'L2_xattn_ckv_w': 4.967,
     'L2_xattn_cdense_w': 4.909,
     'L2_xattn_l_gate': 8.0,
     'L2_xattn_l_up': 8.0,
     'L2_xattn_l_down': 8.0,
     'L3_xattn_l_qkv': 3.206,
     'L3_xattn_l_dense': 8.0,
     'L3_xattn_ckv_w': 8.0,
     'L3_xattn_cdense_w': 8.0,
     'L3_xattn_l_gate': 8.0,
     'L3_xattn_l_up': 8.0,
     'L3_xattn_l_down': 8.0}
    for name, (base, spread) in spreads.items():
        noise = np.random.default_rng([zlib.crc32(name.encode()), seed]).standard_normal(out[name].shape)
        drawn = base * np.exp(spread * noise) if base else spread * noise
        out[name] = jnp.asarray(drawn.astype(out[name].dtype))
    for name, factor in factors.items():
        out[name] = (out[name] * factor).astype(out[name].dtype)
    return out
```

```python
from contextlib import ExitStack

import numpy as np
import concourse.bass as bass
from concourse import mybir

ALU = mybir.AluOpType
ACT = mybir.ActivationFunctionType
F32 = mybir.dt.float32
BF16 = mybir.dt.bfloat16
I32 = mybir.dt.int32
U8 = mybir.dt.uint8
AX_X = mybir.AxisListType.X

P = 128
B, S, D, E = 64, 64, 256, 128
G = 8
GROUPS = B // G
T = G * S
PAIRS = G // 2
DT = D // P
H = 16
L1_HD, L1_INNER, L1_FF = 64, 1024, 1024
JT = L1_INNER // P
HD, CHD = D // H, E // H
FF = 688
FT = -(-FF // P)
FR = FF - (FT - 1) * P
LATE = 48
NEG = -3.3e38
EPS_RMS, EPS_LN = 1e-6, 1e-5

GAINS = ["L0_norm_w", "L0_b_gate", "L1_ln_q_g", "L1_ln_q_b", "L1_ln_ff_g", "L1_ln_ff_b",
         "L2_ln_in_w", "L2_ln_post_cross_w", "L2_ln_post_attn_w",
         "L3_ln_in_w", "L3_ln_post_cross_w", "L3_ln_post_attn_w"]


def projection_order():
    uses = [("in", "x", 0), ("in", "x", 1), ("in", "ctx"), ("mem", 0), ("mem", 1), ("memN", 0), ("memN", 1),
            ("gate", 0), ("gate", 1), ("norm", 0)]
    uses += [("mean", 1), ("norm", 1)]
    for j in range(JT):
        uses += [("l1k", j), ("l1v", j), ("l1q", j)]
    uses += [("mean", 2), ("norm", 2)] + [("l1h", j) for j in range(L1_FF // P)]
    for layer in (2, 3):
        n = 3 * layer - 3
        uses += [("norm", n)]
        uses += [("qk", layer, i) for i in range(4)] + [("v", layer, i) for i in range(2)]
        uses += [("rot", layer, i) for i in range(4)] + [("dense", layer, m) for m in range(DT)]
        uses += [("ck", layer), ("norm", n + 1), ("cq", layer), ("cv", layer)]
        uses += [("cdense", layer, m) for m in range(DT)] + [("norm", n + 2)]
        for j in range(FT):
            uses += [("g", layer, j), ("u", layer, j)]
    uses += [("out", 0), ("out", 1)]
    return {key: n for n, key in enumerate(uses)}


PROJ = projection_order()
L1_U = 1


def SELF_U(layer):
    return 1 + JT + 16 * (layer - 2)


def CROSS_U(layer):
    return SELF_U(layer) + 8


def xattn_kernel(nc, a, out):
    ctx = ExitStack()

    def sb(name, shape, dt=F32):
        return ctx.enter_context(nc.sbuf_tensor(name, shape, dt))

    def pb(name):
        return ctx.enter_context(nc.psum_tensor(name, [P, T], F32))

    sems = []

    def sem(name):
        s = ctx.enter_context(nc.semaphore(name))
        return s

    def turn_sem(name):
        s = sem(name)
        sems.append(s)
        return s

    w_mem = sb("w_mem", [P, D])
    w_gate = sb("w_gate", [P, 2 * DT, D])
    w_q = sb("w_q", [P, DT, L1_INNER])
    w_kv = sb("w_kv", [P, 2 * L1_INNER])
    w_o = sb("w_o", [P, JT, D])
    w_1 = sb("w_1", [P, DT, L1_FF])
    w_2 = sb("w_2", [P, L1_FF // P, D])
    w_qkv, w_dense, w_cq, w_ckv, w_cdense, w_g, w_u, w_down = ({} for _ in range(8))
    for n in (2, 3):
        w_cq[n] = sb(f"w{n}_cq", [P, DT, E])
        w_ckv[n] = sb(f"w{n}_ckv", [P, 2 * E])
        w_cdense[n] = sb(f"w{n}_cdense", [P, D])
        for e in "lv":
            w_qkv[n, e] = sb(f"w{n}_{e}_qkv", [P, DT, 3 * D])
            w_dense[n, e] = sb(f"w{n}_{e}_dense", [P, DT, D])
            w_g[n, e] = sb(f"w{n}_{e}_gate", [P, DT, FF])
            w_u[n, e] = sb(f"w{n}_{e}_up", [P, DT, FF])
            w_down[n, e] = sb(f"w{n}_{e}_down", [P, FT, D])
    gains = sb("gains", [P, len(GAINS), DT])
    gate_scalars = sb("gate_scalars", [P, 2])
    eps = sb("eps", [P, 2])
    ident = sb("ident", [P, P])
    rotate = sb("rotate", [P, P])
    ones = sb("ones", [P, P])
    cos_sin = sb("cos_sin", [P, 2, S])
    head_rows = sb("head_rows", [P, 2, 8])
    ident_bf = sb("ident_bf", [P, P], BF16)
    causal_bf = sb("causal_bf", [P, S], BF16)
    parity_bf = sb("parity_bf", [2, P], BF16)

    xT = sb("xT", [P, DT, T])
    ctxT = sb("ctxT", [P, T])
    xn = sb("xn", [P, DT, T])
    xv = sb("xv", [P, DT, T])
    is_v = sb("is_v", [P, T], BF16)
    is_l = sb("is_l", [P, T], BF16)
    early = sb("early", [P, 2])
    media_raw = sb("media_raw", [2, PAIRS, S], U8)
    media_bias = sb("media_bias", [2, PAIRS, S], BF16)
    Ebuf = sb("Ebuf", [P, 3, T])
    PT = sb("PT", [P, 2, T])
    row_max = sb("row_max", [P, 2, 8])
    row_sum = sb("row_sum", [P, 2, 8])
    row_rcp = sb("row_rcp", [P, 3, 8])
    arena = sb("arena", [P, 7168])
    A_K, A_VS, A_VC, A_QK = 0, 2048, 4096, 5120

    def part(at, *shape):
        n = int(np.prod(shape))
        v = arena[:, at:at + n]
        if len(shape) == 2:
            v = v.rearrange("p (a b) -> p a b", a=shape[0])
        if len(shape) == 3:
            v = v.rearrange("p (a b c) -> p a b c", a=shape[0], b=shape[1])
        if len(shape) == 4:
            v = v.rearrange("p (a b c d) -> p a b c d", a=shape[0], b=shape[1], c=shape[2])
        return v

    x_raw = part(A_VS, PAIRS, D)
    ctx_raw = part(A_VS + 1024, PAIRS, E)
    tt_raw = arena[:, A_VS + 1536:A_VS + 2048].bitcast(I32)
    memT = part(A_QK, DT, T)
    memN = part(A_QK + 1024, 2, 2, D)
    l1_kbd = part(A_K, 2, G, P)
    l1_vbd = part(A_QK, 2, G, P)
    l1_q = part(A_VS, 2, T)
    l1_att = part(A_VS + 1024, 2, T)
    l1_hid = part(A_K, 3, T)
    kbd = part(A_K, 2, 2, 8 * S)
    v_self = part(A_VS, G, 8, 32)
    v_cross = part(A_VC, 2, 2, 8, 32)
    qk = part(A_QK, 4, T)
    silu_g = part(A_K, 2, T)
    hid_l0 = part(A_K + 1024, 2, T)
    hid_v = part(A_QK, 2, T)
    hid_l = [hid_l0[:, 0, :], hid_l0[:, 1, :]]
    out_rows = PT[:, :, :].rearrange("p a t -> p (a t)").rearrange("p (q d) -> p q d", d=D)

    proj_bank = [pb("proj0"), pb("proj1")]
    score_bank = [pb("scores0"), pb("scores1")]
    pt_bank = pb("pt_bank")
    o_bank = pb("o_bank")
    acc = [pb("acc0"), pb("acc1")]

    s_const = sem("s_const")
    s_setup = sem("s_setup")
    s_table = sem("s_table")
    w_loaded = {k: sem(f"w_{k}_loaded") for k in (0, 1, 2, 3)}
    s_first = sem("s_first")

    proj_full = [turn_sem(f"proj{i}_full") for i in range(2)]
    proj_free = [turn_sem(f"proj{i}_free") for i in range(2)]
    acc_full = turn_sem("acc_full")
    acc_free = turn_sem("acc_free")
    scores_ready = turn_sem("scores_ready")
    maxed = turn_sem("maxed")
    shifted = turn_sem("shifted")
    exped = turn_sem("exped")
    summed = turn_sem("summed")
    rcp_ready = turn_sem("rcp_ready")
    probs_ready = turn_sem("probs_ready")
    pt_full = turn_sem("pt_full")
    pt_ready = turn_sem("pt_ready")
    pv_done = turn_sem("pv_done")
    o_taken = turn_sem("o_taken")
    xT_loaded = turn_sem("xT_loaded")
    masks_ready = turn_sem("masks_ready")
    mask_step = turn_sem("mask_step")
    early_ready = turn_sem("early_ready")
    bias_ready = turn_sem("bias_ready")
    mem_ready = turn_sem("mem_ready")
    memN_ready = turn_sem("memN_ready")
    l0_half = turn_sem("l0_half")
    l0_ctx_ready = turn_sem("l0_ctx_ready")
    gate_ready = turn_sem("gate_ready")
    gated = turn_sem("gated")
    kbd_zeroed = turn_sem("kbd_zeroed")
    vbd_zeroed = turn_sem("vbd_zeroed")
    v_zeroed = turn_sem("v_zeroed")
    res_done = turn_sem("res_done")
    centred = turn_sem("centred")
    sq_ready = turn_sem("sq_ready")
    ln_step = turn_sem("ln_step")
    rstd_ready = turn_sem("rstd_ready")
    norm_step = turn_sem("norm_step")
    rstd_v_ready = turn_sem("rstd_v_ready")
    xn_ready = turn_sem("xn_ready")
    xv_ready = turn_sem("xv_ready")
    l1_k_ready = turn_sem("l1_k_ready")
    l1_q_ready = turn_sem("l1_q_ready")
    l1_v_ready = turn_sem("l1_v_ready")
    wo_done = turn_sem("wo_done")
    hid_ready = turn_sem("hid_ready")
    w2_done = turn_sem("w2_done")
    qk_ready = turn_sem("qk_ready")
    cosined = turn_sem("cosined")
    sined = turn_sem("sined")
    roped = turn_sem("roped")
    v_ready = turn_sem("v_ready")
    kbd_ready = turn_sem("kbd_ready")
    cq_ready = turn_sem("cq_ready")
    ck_ready = turn_sem("ck_ready")
    vc_ready = turn_sem("vc_ready")
    silu_ready = turn_sem("silu_ready")
    h_ready = turn_sem("h_ready")
    hl_ready = turn_sem("hl_ready")
    hv_ready = turn_sem("hv_ready")
    down_done = turn_sem("down_done")
    out_ready = turn_sem("out_ready")
    stored = turn_sem("stored")
    next_loaded = turn_sem("next_loaded")

    def bank(key):
        return proj_bank[PROJ[key] % 2]

    def fill(pe, key):
        n = PROJ[key]
        if n >= 2:
            pe.wait_ge(proj_free[n % 2], n // 2)
        return proj_bank[n % 2]

    def full(key):
        return proj_full[PROJ[key] % 2]

    def free(key):
        return proj_free[PROJ[key] % 2]

    def wait_full(eng, key):
        n = PROJ[key]
        eng.wait_ge(proj_full[n % 2], n // 2 + 1)
        return proj_bank[n % 2]

    def gain(name, m):
        return gains[:, GAINS.index(name), m:m + 1]

    def by_batch(v):
        return v.rearrange("p (b s) -> p b s", s=S)

    def load_group(q, i, done):
        rows = a["x"].rearrange("(g t p) d -> g p t d", g=GROUPS, p=P)[i]
        q.dma_start(x_raw, rows).then_inc(done, 16)
        rows = a["ctx"].rearrange("(g t p) d -> g p t d", g=GROUPS, p=P)[i]
        q.dma_start(ctx_raw, rows).then_inc(done, 16)
        q.dma_start(tt_raw, a["types"].rearrange("(g o t) -> g o t", g=GROUPS, o=1)[i].broadcast_to([P, T])).then_inc(done, 16)
        q.dma_start(media_raw[:, :, :].bitcast(I32), a["media_mask"].rearrange("(g b r) s -> g r b s", g=GROUPS, r=2)[i]).then_inc(done, 16)

    with nc.Block() as block:
        @block.sync
        def _(q):
            load_group(q, 0, s_first)
            q.dma_start(ident[:, :], a["c_ident"]).then_inc(s_const, 16)
            q.dma_start(rotate[:, :], a["c_rotate"]).then_inc(s_const, 16)
            q.dma_start(head_rows[:, :, :], a["c_head_rows"]).then_inc(s_const, 16)
            q.dma_start(Ebuf[:, 0, 0:S], a["c_causal"]).then_inc(s_const, 16)
            q.dma_start(Ebuf[0:S, 1, 0:2 * P], a["c_cos_sin"]).then_inc(s_const, 16)
            q.dma_start(Ebuf[0:S, 2, 0:S].bitcast(I32), a["positions"].broadcast_to([S, S])).then_inc(s_const, 16)
            q.dma_start(Ebuf[0:S, 2, S:S + 1], a["c_index"]).then_inc(s_const, 16)
            q.dma_start(Ebuf[0:2, 2, 128:256], a["c_parity"]).then_inc(s_const, 16)
            q.dma_start(gate_scalars[:, 0:1], a["L1_attn_gate"].rearrange("(o n) -> o n", o=1).broadcast_to([P, 1])).then_inc(s_const, 16)
            q.dma_start(gate_scalars[:, 1:2], a["L1_ff_gate"].rearrange("(o n) -> o n", o=1).broadcast_to([P, 1])).then_inc(s_const, 16)
            for n, name in enumerate(GAINS):
                with nc.allow_non_contiguous_dma(reason="one word per row, once"):
                    q.dma_start(gains[:, n, :], a[name].rearrange("(m p) -> p m", p=P)).then_inc(s_const, 16)

            def load_w(dst, src, k):
                q.dma_start(dst, src).then_inc(w_loaded[k], 16)

            def tiles(v):
                return v.rearrange("(t p) n -> p t n", p=P)

            load_w(w_mem[:, :], a["L0_W_memT"], 0)
            load_w(w_gate[:, :, :], tiles(a["L0_W_gateT"]), 0)
            load_w(w_kv[:, :], a["L1_Wkv"], 1)
            load_w(w_q[:, :, :], tiles(a["L1_Wq"]), 1)
            load_w(w_o[:, :, :], tiles(a["L1_Wo"]), 1)
            load_w(w_1[:, :, :], tiles(a["L1_W1"]), 1)
            load_w(w_2[:, :, :], tiles(a["L1_W2"]), 1)
            for n in (2, 3):
                for e in "lv":
                    load_w(w_qkv[n, e][:, :, :], tiles(a[f"L{n}_{e}_qkv"]), n)
                    load_w(w_dense[n, e][:, :, :], tiles(a[f"L{n}_{e}_dense"]), n)
                load_w(w_cq[n][:, :, :], tiles(a[f"L{n}_cq_w"]), n)
                load_w(w_ckv[n][:, :], a[f"L{n}_ckv_w"], n)
                load_w(w_cdense[n][:, :], a[f"L{n}_cdense_w"], n)
                for e in "lv":
                    load_w(w_g[n, e][:, :, :], tiles(a[f"L{n}_{e}_gate"]), n)
                    load_w(w_u[n, e][:, :, :], tiles(a[f"L{n}_{e}_up"]), n)
                    down = a[f"L{n}_{e}_down"]
                    load_w(w_down[n, e][:, 0:FT - 1, :], tiles(down[0:(FT - 1) * P, :]), n)
                    load_w(w_down[n, e][0:FR, FT - 1, :], down[(FT - 1) * P:FF, :], n)

        @block.vector
        def _(dve):
            nc.vector.memset(ones[:, :], 1.0).then_inc(s_setup, 1)
            nc.vector.memset(eps[:, 0:1], EPS_RMS).then_inc(s_setup, 1)
            nc.vector.memset(eps[:, 1:2], EPS_LN).then_inc(s_setup, 1)
            dve.wait_ge(s_const, 16 * (10 + len(GAINS)))
            nc.vector.tensor_copy(ident_bf[:, :], ident[:, :]).then_inc(s_setup, 1)
            nc.vector.tensor_copy(causal_bf[:, :], Ebuf[:, 0, 0:S]).then_inc(s_setup, 1)
            nc.vector.tensor_copy(parity_bf[:, :], Ebuf[0:2, 2, 128:256]).then_inc(s_setup, 1)
            pos, wrap, hot = Ebuf[0:S, 2, 256:256 + S], Ebuf[0:S, 2, 320:320 + S], Ebuf[0:S, 2, 384:384 + S]
            nc.vector.tensor_copy(pos, Ebuf[0:S, 2, 0:S].bitcast(I32)).then_inc(s_table, 1)
            dve.wait_ge(s_table, 1)
            nc.vector.tensor_scalar(wrap, pos, 0.0, float(S), ALU.is_lt, ALU.mult).then_inc(s_table, 1)
            dve.wait_ge(s_table, 2)
            nc.vector.tensor_tensor(pos, pos, wrap, ALU.add).then_inc(s_table, 1)
            dve.wait_ge(s_table, 3)
            nc.vector.tensor_scalar(wrap, pos, 0.0, float(S - 1), ALU.max, ALU.min).then_inc(s_table, 1)
            dve.wait_ge(s_table, 4)
            nc.vector.tensor_scalar(hot, wrap, Ebuf[0:S, 2, S:S + 1], None, ALU.is_equal).then_inc(s_table, 1)
            dve.wait_ge(s_table, 6)
            nc.vector.tensor_copy(cos_sin[:, :, :], proj_bank[0][:, 0:2 * S].rearrange("p (a s) -> p a s", a=2)).then_inc(s_table, 1)
            dve.wait_ge(s_table, 7)
            dve.wait_ge(s_first, 64)

        @block.tensor
        def _(pe):
            pe.wait_ge(s_table, 5)
            for n in range(2):
                last = nc.tensor.matmul(proj_bank[0][:, n * S:(n + 1) * S], Ebuf[0:S, 1, n * P:(n + 1) * P],
                                        Ebuf[0:S, 2, 384:384 + S], start=True, stop=True)
            last.then_inc(s_table, 1)

        @block.scalar
        def _(act):
            act.wait_ge(s_const, 16 * (10 + len(GAINS)))
            nc.scalar.activation(gate_scalars[:, :], gate_scalars[:, :], ACT.Tanh).then_inc(s_setup, 1)

        @block.gpsimd
        def _(pool):
            pool.wait_ge(s_setup, 7)

    with nc.Fori(0, GROUPS) as turn:
        with nc.Block() as block:
            @block.sync
            def _(q):
                q.wait_ge(pv_done, SELF_U(3) + 8)
                load_group(q, (turn + 1) % GROUPS, next_loaded)
                q.wait_ge(out_ready, 2)
                q.dma_start(out.rearrange("(g t p) d -> g p t d", g=GROUPS, p=P)[turn], out_rows).then_inc(stored, 16)
                q.wait_ge(stored, 16)
                q.wait_ge(next_loaded, 64)

            @block.tensor
            def _(pe):
                mm = nc.tensor.matmul

                def transposes_unit(u, cols):
                    pe.wait_ge(probs_ready, u + 1)
                    if u >= 1:
                        pe.wait_ge(pt_ready, u)
                    for c in range(cols // P):
                        last = nc.tensor.transpose(pt_bank[:, c * P:(c + 1) * P], Ebuf[:, u % 3, c * P:(c + 1) * P], ident[:, :])
                    last.then_inc(pt_full, 1)

                def norm_sums(n, src_ready, count):
                    b = fill(pe, ("norm", n))
                    for m in range(DT):
                        pe.wait_ge(src_ready, count - DT + m + 1)
                        last = mm(b[:, :], ones[:, :], Ebuf[:, m, :], start=(m == 0), stop=(m == DT - 1))
                    last.then_inc(full(("norm", n)), 1)

                def mean_sums(n):
                    b = fill(pe, ("mean", n))
                    pe.wait_ge(res_done, 2 * n)
                    for m in range(DT):
                        last = mm(b[:, :], ones[:, :], xT[:, m, :], start=(m == 0), stop=(m == DT - 1))
                    last.then_inc(full(("mean", n)), 1)

                for m in range(DT):
                    b = fill(pe, ("in", "x", m))
                    for t in range(PAIRS):
                        last = nc.tensor.transpose(b[:, t * P:(t + 1) * P], x_raw[:, t, m * P:(m + 1) * P], ident[:, :])
                    last.then_inc(full(("in", "x", m)), 1)
                b = fill(pe, ("in", "ctx"))
                for t in range(PAIRS):
                    last = nc.tensor.transpose(b[:, t * P:(t + 1) * P], ctx_raw[:, t, :], ident[:, :])
                last.then_inc(full(("in", "ctx")), 1)

                pe.wait_ge(w_loaded[0], 32)
                pe.wait_ge(xT_loaded, 3)
                for m in range(DT):
                    b = fill(pe, ("mem", m))
                    mm(b[:, :], w_mem[:, m * P:(m + 1) * P], ctxT[:, :], start=True, stop=True).then_inc(full(("mem", m)), 1)
                for i in range(2):
                    b = fill(pe, ("memN", i))
                    for r in range(2):
                        for e in range(2):
                            n = 2 * (2 * i + e) + r
                            last = mm(b[64 * e:64 * e + 64, r * D:(r + 1) * D], ctxT[:, n * S:(n + 1) * S], w_mem[:, :],
                                      start=True, stop=True)
                    last.then_inc(full(("memN", i)), 1)
                pe.wait_ge(mem_ready, DT)
                for p in range(PAIRS):
                    for r in range(2):
                        n = 2 * p + r
                        for m in range(DT):
                            last = mm(score_bank[0][64 * r:64 * r + 64, p * S:(p + 1) * S], xT[:, m, n * S:(n + 1) * S],
                                      memT[:, m, n * S:(n + 1) * S], start=(m == 0), stop=(m == DT - 1))
                last.then_inc(scores_ready, 1)
                transposes_unit(0, PAIRS * S)
                pe.wait_ge(pt_ready, 1)
                pe.wait_ge(memN_ready, 2)
                for e in range(2):
                    for m in range(DT):
                        for i in range(2):
                            for r in range(2):
                                n, at = 2 * (2 * i + e) + r, i * P + r * S
                                last = mm(acc[m][:, n * S:(n + 1) * S], memN[64 * e:64 * e + 64, i, r, m * P:(m + 1) * P],
                                          PT[64 * e:64 * e + 64, 0, at:at + S], start=True, stop=True)
                    if e == 0:
                        last.then_inc(l0_half, 1)
                        pe.wait_ge(l0_half, 1)
                last.then_inc(pv_done, 1)
                for m in range(DT):
                    b = fill(pe, ("gate", m))
                    for k in range(DT):
                        mm(b[:, :], w_gate[:, k, m * P:(m + 1) * P], xT[:, k, :], start=(k == 0), stop=False)
                    for k in range(DT):
                        pe.wait_ge(l0_ctx_ready, k + 1)
                        last = mm(b[:, :], w_gate[:, DT + k, m * P:(m + 1) * P], xv[:, k, :], start=False, stop=(k == DT - 1))
                    last.then_inc(full(("gate", m)), 1)
                norm_sums(0, sq_ready, 2)

                mean_sums(1)
                norm_sums(1, sq_ready, 4)
                pe.wait_ge(w_loaded[1], 16 * 5)
                pe.wait_ge(bias_ready, 1)
                for j in range(JT + 2):
                    if j < JT:
                        b = fill(pe, ("l1k", j))
                        mm(b[:, :], w_kv[:, j * P:(j + 1) * P], ctxT[:, :], start=True, stop=True).then_inc(full(("l1k", j)), 1)
                        b = fill(pe, ("l1v", j))
                        for p in range(PAIRS):
                            last = mm(b[:, p * P:(p + 1) * P], ctxT[:, p * P:(p + 1) * P],
                                      w_kv[:, L1_INNER + j * P:L1_INNER + (j + 1) * P], start=True, stop=True)
                        last.then_inc(full(("l1v", j)), 1)
                        b = fill(pe, ("l1q", j))
                        for k in range(DT):
                            if j == 0:
                                pe.wait_ge(xn_ready, k + 1)
                            last = mm(b[:, :], w_q[:, k, j * P:(j + 1) * P], xn[:, k, :], start=(k == 0), stop=(k == DT - 1))
                        last.then_inc(full(("l1q", j)), 1)
                    if 1 <= j <= JT:
                        transposes_unit(L1_U + j - 1, T)
                    if j < JT:
                        u = L1_U + j
                        pe.wait_ge(shifted, u - 1)
                        pe.wait_ge(l1_k_ready, j + 1)
                        pe.wait_ge(l1_q_ready, j + 1)
                        sc = score_bank[u % 2]
                        mm(sc[:, :].rearrange("p (b h s) -> p b h s", b=PAIRS, h=2), parity_bf[:, :],
                           media_bias[:, :, :].unsqueeze(2).broadcast_to([2, PAIRS, 2, S]), start=True, stop=True)
                        for p in range(PAIRS):
                            for r in range(2):
                                n = 2 * p + r
                                last = mm(sc[64 * r:64 * r + 64, p * P:(p + 1) * P], l1_q[:, j % 2, n * S:(n + 1) * S],
                                          l1_kbd[:, j % 2, n, :], start=False, stop=True, skip_group_check=True)
                        last.then_inc(scores_ready, 1)
                    if 1 <= j <= JT:
                        u = L1_U + j - 1
                        pe.wait_ge(pt_ready, u + 1)
                        pe.wait_ge(l1_v_ready, j)
                        pe.wait_ge(o_taken, u)
                        for n in range(G):
                            last = mm(o_bank[:, n * S:(n + 1) * S], l1_vbd[:, (j - 1) % 2, n, :],
                                      PT[:, u % 2, n * S:(n + 1) * S], start=True, stop=True)
                        last.then_inc(pv_done, 1)
                    if j >= 2:
                        t = j - 2
                        pe.wait_ge(o_taken, L1_U + t + 1)
                        if t == 0:
                            pe.wait_ge(acc_free, 1)
                        for m in range(DT):
                            last = mm(acc[m][:, :], w_o[:, t, m * P:(m + 1) * P], l1_att[:, t % 2, :],
                                      start=(t == 0), stop=(t == JT - 1))
                        last.then_inc(wo_done, 1)
                        if t == JT - 1:
                            pass
                mean_sums(2)
                norm_sums(2, sq_ready, 6)
                NF = L1_FF // P
                for j in range(NF + 1):
                    if j < NF:
                        b = fill(pe, ("l1h", j))
                        for k in range(DT):
                            if j == 0:
                                pe.wait_ge(xn_ready, 2 + k + 1)
                            last = mm(b[:, :], w_1[:, k, j * P:(j + 1) * P], xn[:, k, :], start=(k == 0), stop=(k == DT - 1))
                        last.then_inc(full(("l1h", j)), 1)
                    if j >= 1:
                        t = j - 1
                        pe.wait_ge(hid_ready, t + 1)
                        if t == 0:
                            pe.wait_ge(acc_free, 2)
                        for m in range(DT):
                            last = mm(acc[m][:, :], w_2[:, t, m * P:(m + 1) * P], l1_hid[:, t % 3, :],
                                      start=(t == 0), stop=(t == NF - 1))
                        last.then_inc(w2_done, 1)

                def experts(b, rows, w_l, w_v, src_l, src_v, every, last_stop=True):
                    k_rows = P
                    for k in range(len(w_l)):
                        mm(b[0:rows, :], w_l[k], src_l[k], start=(k == 0), stop=(not every and k == len(w_l) - 1))
                    for k in range(len(w_v)):
                        if every:
                            last = mm(b[0:rows, :], w_v[k], src_v[k], start=False, stop=(k == len(w_v) - 1))
                        else:
                            last = mm(by_batch(b[0:rows, :])[:, :, LATE:S], w_v[k], by_batch(src_v[k])[:, :, LATE:S],
                                      start=False, stop=(k == len(w_v) - 1), skip_group_check=True)
                    return last

                def layer(n, every):
                    li = n - 2
                    pe.wait_ge(w_loaded[n], 16 * (4 + 3 + 8))
                    norm_sums(3 * n - 3, sq_ready, 2 * (3 * n - 3) + 2)
                    xn_base, xv_base = 4 + 6 * li, 4 * li
                    pe.wait_ge(xn_ready, xn_base + 2)
                    pe.wait_ge(xv_ready, xv_base + 2)
                    for i in range(4):
                        b = fill(pe, ("qk", n, i))
                        at = (i // 2) * P + (D if i % 2 == 0 else 0)
                        experts(b, P, [w_qkv[n, "l"][:, k, at:at + P] for k in range(DT)],
                                [w_qkv[n, "v"][:, k, at:at + P] for k in range(DT)],
                                [xn[:, k, :] for k in range(DT)], [xv[:, k, :] for k in range(DT)], every
                                ).then_inc(full(("qk", n, i)), 1)
                    for i in range(2):
                        b = fill(pe, ("v", n, i))
                        for c in range(2):
                            p = 2 * i + c
                            for k, (e, src) in enumerate((e, src) for e, src in (("l", xn), ("v", xv)) for _ in range(DT)):
                                last = mm(b[:, c * D:(c + 1) * D], src[:, k % DT, p * P:(p + 1) * P],
                                          w_qkv[n, e][:, k % DT, 2 * D:3 * D], start=(k == 0), stop=(k == 3))
                        last.then_inc(full(("v", n, i)), 1)
                    for i in range(4):
                        b = fill(pe, ("rot", n, i))
                        pe.wait_ge(qk_ready, 4 * li + i + 1)
                        mm(b[:, :], rotate[:, :], qk[:, i, :], start=True, stop=True).then_inc(full(("rot", n, i)), 1)

                    def self_scores(i):
                        u, t, p = SELF_U(n) + i, i // PAIRS, i % PAIRS
                        pe.wait_ge(shifted, u - 1)
                        pe.wait_ge(roped, 4 * li + 2 * t + 2)
                        pe.wait_ge(kbd_ready, 12 * li + i + 1)
                        sc = score_bank[u % 2]
                        mm(sc[:, :].rearrange("p (h s) -> p h s", h=8), ident_bf[:, :],
                           causal_bf[:, :].unsqueeze(1).broadcast_to([P, 8, S]), start=True, stop=True)
                        for r in range(2):
                            b = 2 * p + r
                            last = mm(sc[64 * r:64 * r + 64, :], qk[:, 2 * t + 1, b * S:(b + 1) * S], kbd[:, i % 2, r, :],
                                      start=False, stop=True, skip_group_check=True)
                        last.then_inc(scores_ready, 1)

                    def self_pv(i):
                        u, t, p = SELF_U(n) + i, i // PAIRS, i % PAIRS
                        pe.wait_ge(pt_ready, u + 1)
                        pe.wait_ge(o_taken, u)
                        for c in range(4):
                            for r in range(2):
                                last = mm(o_bank[32 * c:32 * c + 32, r * S:(r + 1) * S], v_self[:, 2 * p + r, 4 * t + c, :],
                                          PT[:, u % 2, c * P + r * S:c * P + (r + 1) * S], start=True, stop=True)
                        last.then_inc(pv_done, 1)

                    pe.wait_ge(v_ready, 2 * li + 2)
                    for i in range(8 + 3):
                        if i < 8:
                            self_scores(i)
                        if 2 <= i < 10:
                            transposes_unit(SELF_U(n) + i - 2, T)
                        if i >= 3:
                            self_pv(i - 3)
                    pe.wait_ge(o_taken, SELF_U(n) + 8)
                    for m in range(DT):
                        b = fill(pe, ("dense", n, m))
                        experts(b, P, [w_dense[n, "l"][:, k, m * P:(m + 1) * P] for k in range(DT)],
                                [w_dense[n, "v"][:, k, m * P:(m + 1) * P] for k in range(DT)],
                                [xn[:, k, :] for k in range(DT)], [xv[:, k, :] for k in range(DT)], every
                                ).then_inc(full(("dense", n, m)), 1)
                    b = fill(pe, ("ck", n))
                    mm(b[:, :], w_ckv[n][:, 0:E], ctxT[:, :], start=True, stop=True).then_inc(full(("ck", n)), 1)
                    norm_sums(3 * n - 2, sq_ready, 2 * (3 * n - 2) + 2)
                    b = fill(pe, ("cq", n))
                    for k in range(DT):
                        pe.wait_ge(xn_ready, xn_base + 3 + k)
                        last = mm(b[:, :], w_cq[n][:, k, :], xn[:, k, :], start=(k == 0), stop=(k == DT - 1))
                    last.then_inc(full(("cq", n)), 1)
                    b = fill(pe, ("cv", n))
                    for p in range(PAIRS):
                        last = mm(b[:, p * P:(p + 1) * P], ctxT[:, p * P:(p + 1) * P], w_ckv[n][:, E:2 * E], start=True, stop=True)
                    last.then_inc(full(("cv", n)), 1)

                    def cross_scores(i):
                        u, p, r8 = CROSS_U(n) + i, i // 2, i % 2
                        pe.wait_ge(shifted, u - 1)
                        pe.wait_ge(kbd_ready, 12 * li + 8 + p + 1)
                        sc = score_bank[u % 2]
                        for r in range(2):
                            b = 2 * p + r
                            last = mm(sc[64 * r:64 * r + 64, :], qk[64 * r8:64 * r8 + 64, 0, b * S:(b + 1) * S],
                                      kbd[64 * r8:64 * r8 + 64, p % 2, r, :], start=True, stop=True)
                        last.then_inc(scores_ready, 1)

                    def cross_pv(i):
                        u, p, r8 = CROSS_U(n) + i, i // 2, i % 2
                        pe.wait_ge(pt_ready, u + 1)
                        pe.wait_ge(o_taken, u)
                        pe.wait_ge(vc_ready, 4 * li + p + 1)
                        for r in range(2):
                            for c in range(4):
                                at = 64 * r8 + 32 * (c // 2)
                                last = mm(o_bank[at:at + 32, r * S:(r + 1) * S], v_cross[:, p % 2, r, 4 * r8 + c, :],
                                          PT[:, u % 2, c * P + r * S:c * P + (r + 1) * S], start=(c % 2 == 0), stop=(c % 2 == 1))
                        last.then_inc(pv_done, 1)

                    pe.wait_ge(cq_ready, li + 1)
                    for i in range(8 + 3):
                        if i < 8:
                            cross_scores(i)
                        if 2 <= i < 10:
                            transposes_unit(CROSS_U(n) + i - 2, T)
                        if i >= 3:
                            cross_pv(i - 3)
                    pe.wait_ge(o_taken, CROSS_U(n) + 8)
                    for m in range(DT):
                        b = fill(pe, ("cdense", n, m))
                        mm(b[:, :], w_cdense[n][:, m * P:(m + 1) * P], xv[:, 0, :], start=True, stop=True
                           ).then_inc(full(("cdense", n, m)), 1)
                    norm_sums(3 * n - 1, sq_ready, 2 * (3 * n - 1) + 2)
                    pe.wait_ge(xn_ready, xn_base + 6)
                    pe.wait_ge(xv_ready, xv_base + 4)
                    for j in range(FT + 1):
                        if j < FT:
                            rows = P if j < FT - 1 else FR
                            for key, w in (("g", w_g), ("u", w_u)):
                                b = fill(pe, (key, n, j))
                                experts(b, rows, [w[n, "l"][:, k, j * P:j * P + rows] for k in range(DT)],
                                        [w[n, "v"][:, k, j * P:j * P + rows] for k in range(DT)],
                                        [xn[:, k, :] for k in range(DT)], [xv[:, k, :] for k in range(DT)], every
                                        ).then_inc(full((key, n, j)), 1)
                        if j >= 1:
                            t = j - 1
                            rows = P if t < FT - 1 else FR
                            pe.wait_ge(hl_ready, FT * li + t + 1)
                            pe.wait_ge(hv_ready, FT * li + t + 1)
                            if t == 0:
                                pe.wait_ge(acc_free, 3 + li)
                            for m in range(DT):
                                mm(acc[m][:, :], w_down[n, "l"][0:rows, t, m * P:(m + 1) * P], hid_l[t % 2][0:rows, :],
                                   start=(t == 0), stop=(not every and t == FT - 1), skip_group_check=every)
                                wv, hv = w_down[n, "v"][0:rows, t, m * P:(m + 1) * P], hid_v[0:rows, t % 2, :]
                                if every:
                                    last = mm(acc[m][:, :], wv, hv, start=False, stop=(t == FT - 1), skip_group_check=True)
                                else:
                                    last = mm(by_batch(acc[m][:, :])[:, :, LATE:S], wv, by_batch(hv)[:, :, LATE:S],
                                              start=False, stop=(t == FT - 1), skip_group_check=True)
                            last.then_inc(down_done, 1)

                pe.wait_ge(early_ready, 2)
                any_early = pe.value_load(early[0:1, 1:2].bitcast(I32))
                with pe.If(any_early > 0):
                    layer(2, True)
                    layer(3, True)
                with pe.Else():
                    layer(2, False)
                    layer(3, False)

                pe.wait_ge(res_done, 18)
                for i in range(2):
                    b = fill(pe, ("out", i))
                    for c in range(2):
                        for m in range(DT):
                            t = 2 * i + c
                            last = nc.tensor.transpose(b[:, c * D + m * P:c * D + (m + 1) * P], xT[:, m, t * P:(t + 1) * P], ident[:, :])
                    last.then_inc(full(("out", i)), 1)

            @block.scalar
            def _(act):
                A = nc.scalar.activation

                def copy(dst, src, key, ready):
                    A(dst, src, ACT.Copy).then_inc(ready, 1)

                def exp_unit(u, cols, scale):
                    act.wait_ge(shifted, u + 1)
                    A(Ebuf[:, u % 3, 0:cols], Ebuf[:, u % 3, 0:cols], ACT.Exp, scale=scale).then_inc(exped, 1)

                def pt_copy(u, cols):
                    act.wait_ge(pt_full, u + 1)
                    if u >= 2:
                        act.wait_ge(pv_done, u - 1)
                    A(PT[:, u % 2, 0:cols], pt_bank[:, 0:cols], ACT.Copy).then_inc(pt_ready, 1)

                def squares(src, ready, count):
                    for m in range(DT):
                        act.wait_ge(ready, count - DT + m + 1)
                        A(Ebuf[:, m, :], src[:, m, :], ACT.Square).then_inc(sq_ready, 1)

                def rstd(n, which):
                    b = wait_full(act, ("norm", n))
                    A(Ebuf[:, 2, :], b[:, :], ACT.Ln, scale=1.0 / D, bias=eps[:, which:which + 1]).then_inc(free(("norm", n)), 1)
                    act.wait_ge(free(("norm", n)), PROJ["norm", n] // 2 + 1)
                    A(Ebuf[:, 2, :], Ebuf[:, 2, :], ACT.Exp, scale=-0.5).then_inc(rstd_ready, 1)

                for m in range(DT):
                    b = wait_full(act, ("in", "x", m))
                    A(xT[:, m, :], b[:, :], ACT.Copy).then_inc(xT_loaded, 1)
                    act.wait_ge(xT_loaded, m + 1)
                    act.sem_inc(free(("in", "x", m)), 1)
                b = wait_full(act, ("in", "ctx"))
                A(ctxT[:, :], b[:, :], ACT.Copy).then_inc(xT_loaded, 1)
                act.wait_ge(xT_loaded, 3)
                act.sem_inc(free(("in", "ctx")), 1)
                for m in range(DT):
                    b = wait_full(act, ("mem", m))
                    A(memT[:, m, :], b[:, :], ACT.Copy).then_inc(mem_ready, 1)
                    act.wait_ge(mem_ready, m + 1)
                    act.sem_inc(free(("mem", m)), 1)
                exp_unit(0, PAIRS * S, D ** -0.5)
                pt_copy(0, PAIRS * S)
                act.wait_ge(pv_done, 1)
                for m in range(DT):
                    A(xv[:, m, :], acc[m][:, :], ACT.Copy).then_inc(l0_ctx_ready, 1)
                act.wait_ge(l0_ctx_ready, 2)
                act.sem_inc(acc_free, 1)
                act.sem_inc(o_taken, 1)
                for m in range(DT):
                    b = wait_full(act, ("gate", m))
                    A(xn[:, m, :], b[:, :], ACT.Sigmoid, bias=gain("L0_b_gate", m)).then_inc(gate_ready, 1)
                    act.wait_ge(gate_ready, m + 1)
                    act.sem_inc(free(("gate", m)), 1)
                squares(xT, gated, 4)
                rstd(0, 0)
                squares(xn, centred, 2)
                rstd(1, 1)
                act.wait_ge(kbd_zeroed, 1)
                for j in range(JT + 1):
                    if j < JT:
                        b = wait_full(act, ("l1k", j))
                        if j >= 2:
                            act.wait_ge(scores_ready, L1_U + j - 1)
                        for r in range(2):
                            last = A(l1_kbd[64 * r:64 * r + 64, j % 2, :, 64 * r:64 * r + 64], by_batch(b[64 * r:64 * r + 64, :]), ACT.Copy)
                            if r == 0:
                                continue
                        last.then_inc(l1_k_ready, 1)
                        act.wait_ge(l1_k_ready, j + 1)
                        act.sem_inc(free(("l1k", j)), 1)
                        b = wait_full(act, ("l1q", j))
                        A(l1_q[:, j % 2, :], b[:, :], ACT.Copy).then_inc(l1_q_ready, 1)
                        act.wait_ge(l1_q_ready, j + 1)
                        act.sem_inc(free(("l1q", j)), 1)
                    if j >= 1:
                        pt_copy(L1_U + j - 1, T)
                    if j < JT:
                        exp_unit(L1_U + j, T, L1_HD ** -0.5)
                squares(xn, centred, 4)
                rstd(2, 1)
                for j in range(L1_FF // P):
                    b = wait_full(act, ("l1h", j))
                    if j >= 3:
                        act.wait_ge(w2_done, j - 2)
                    A(l1_hid[:, j % 3, :], b[:, :], ACT.Gelu).then_inc(hid_ready, 1)
                    act.wait_ge(hid_ready, j + 1)
                    act.sem_inc(free(("l1h", j)), 1)

                for n in (2, 3):
                    li = n - 2
                    squares(xT, res_done, 6 * n - 6)
                    rstd(3 * n - 3, 0)
                    for i in range(4):
                        b = wait_full(act, ("qk", n, i))
                        A(qk[:, i, :], b[:, :], ACT.Copy).then_inc(qk_ready, 1)
                        act.wait_ge(qk_ready, 4 * li + i + 1)
                        act.sem_inc(free(("qk", n, i)), 1)
                    act.wait_ge(v_zeroed, 1)
                    for i in range(2):
                        b = wait_full(act, ("v", n, i))
                        for r in range(2):
                            for e in range(2):
                                src = b[64 * r:64 * r + 64, :].rearrange("p (c h e d) -> p c h e d", c=2, h=8, e=2)[:, :, :, e, :]
                                dst = v_self[64 * e:64 * e + 64, 4 * i + r:4 * i + r + 3:2, :, 16 * e:16 * e + 16]
                                last = A(dst, src, ACT.Copy)
                        last.then_inc(v_ready, 1)
                        act.wait_ge(v_ready, 2 * li + i + 1)
                        act.sem_inc(free(("v", n, i)), 1)
                    for i in range(8 + 2):
                        if i < 8:
                            exp_unit(SELF_U(n) + i, T, HD ** -0.5)
                        if i >= 2:
                            pt_copy(SELF_U(n) + i - 2, T)
                    b = wait_full(act, ("ck", n))
                    A(qk[:, 1, :], b[:, :], ACT.Copy).then_inc(ck_ready, 1)
                    act.wait_ge(ck_ready, li + 1)
                    act.sem_inc(free(("ck", n)), 1)
                    squares(xT, res_done, 6 * n - 4)
                    rstd(3 * n - 2, 0)
                    b = wait_full(act, ("cq", n))
                    A(qk[:, 0, :], b[:, :], ACT.Copy).then_inc(cq_ready, 1)
                    act.wait_ge(cq_ready, li + 1)
                    act.sem_inc(free(("cq", n)), 1)
                    b = wait_full(act, ("cv", n))

                    def cross_values(p):
                        if p >= 2:
                            act.wait_ge(pv_done, CROSS_U(n) + 2 * p - 2)
                        for r in range(2):
                            for e in range(2):
                                src = b[64 * r:64 * r + 64, p * P:(p + 1) * P].rearrange("p (h f e d) -> p h f e d", h=4, f=2, e=2)[:, :, :, e, :]
                                dst = v_cross[64 * e:64 * e + 64, p % 2, r, :, :].rearrange("p (h f) c -> p h f c", f=2)
                                for f in range(2):
                                    last = A(dst[:, :, f, 16 * f + 8 * e:16 * f + 8 * e + 8], src[:, :, f, :], ACT.Copy)
                        last.then_inc(vc_ready, 1)

                    cross_values(0)
                    for i in range(8 + 2):
                        if i < 8:
                            exp_unit(CROSS_U(n) + i, T, CHD ** -0.5)
                            if i % 2 == 1 and i // 2 + 1 < PAIRS and i // 2 + 1 < 2:
                                cross_values(i // 2 + 1)
                        if i >= 2:
                            pt_copy(CROSS_U(n) + i - 2, T)
                            if i % 2 == 1 and 2 <= i // 2 + 0 < PAIRS:
                                cross_values(i // 2)
                    act.wait_ge(vc_ready, 4 * li + 4)
                    act.sem_inc(free(("cv", n)), 1)
                    squares(xT, res_done, 6 * n - 2)
                    rstd(3 * n - 1, 0)
                    for j in range(FT):
                        rows = P if j < FT - 1 else FR
                        b = wait_full(act, ("g", n, j))
                        if j >= 2:
                            act.wait_ge(hv_ready, FT * li + j - 1)
                            act.wait_ge(hl_ready, FT * li + j - 1)
                        A(silu_g[0:rows, j % 2, :], b[0:rows, :], ACT.Silu).then_inc(silu_ready, 1)
                        act.wait_ge(silu_ready, FT * li + j + 1)
                        act.sem_inc(free(("g", n, j)), 1)
                for i in range(2):
                    b = wait_full(act, ("out", i))
                    A(out_rows[:, 2 * i:2 * i + 2, :], b[:, :].rearrange("p (q d) -> p q d", d=D), ACT.Copy).then_inc(out_ready, 1)

            @block.vector
            def _(dve):
                V = nc.vector

                def groups(v, g):
                    return v.rearrange("p (g s) -> p g s", s=S)

                def shift_unit(u, g):
                    sc = groups(score_bank[u % 2][:, 0:g * S], g)
                    dve.wait_ge(scores_ready, u + 1)
                    if u >= 2:
                        dve.wait_ge(shifted, u - 1)
                    V.reduce_max(row_max[:, u % 2, 0:g], sc, AX_X).then_inc(maxed, 1)
                    dve.wait_ge(maxed, u + 1)
                    if u >= 3:
                        dve.wait_ge(pt_full, u - 2)
                    V.tensor_tensor(groups(Ebuf[:, u % 3, 0:g * S], g), sc,
                                    row_max[:, u % 2, 0:g].unsqueeze(2).broadcast_to([P, g, S]), ALU.subtract).then_inc(shifted, 1)

                def sum_unit(u, g):
                    dve.wait_ge(exped, u + 1)
                    if u >= 2:
                        dve.wait_ge(rcp_ready, u - 1)
                    V.reduce_sum(row_sum[:, u % 2, 0:g], groups(Ebuf[:, u % 3, 0:g * S], g), AX_X).then_inc(summed, 1)
                    dve.wait_ge(summed, u + 1)
                    if u >= 3:
                        dve.wait_ge(probs_ready, u - 2)
                    V.reciprocal(row_rcp[:, u % 3, 0:g], row_sum[:, u % 2, 0:g]).then_inc(rcp_ready, 1)

                def residual(key, m):
                    b = wait_full(dve, key)
                    V.tensor_tensor(xT[:, m, :], b[:, :], xT[:, m, :], ALU.add).then_inc(res_done, 1)

                def plain_norm(n, name, dst, ready):
                    dve.wait_ge(rstd_ready, n + 1)
                    for m in range(DT):
                        V.scalar_tensor_tensor(out=dst[:, m, :], in0=xT[:, m, :], scalar=gain(name, m), in1=Ebuf[:, 2, :],
                                               op0=ALU.mult, op1=ALU.mult).then_inc(ready, 1)

                V.tensor_scalar(Ebuf[:, 0, :], tt_raw, 1.0, None, ALU.is_equal).then_inc(mask_step, 1)
                V.tensor_scalar(media_bias[:, :, :], media_raw[:, :, :], -NEG, NEG, ALU.mult, ALU.add).then_inc(bias_ready, 1)
                V.memset(by_batch(is_v[:, :])[:, :, S - 1:S], 0.0).then_inc(mask_step, 1)
                dve.wait_ge(mask_step, 2)
                same = by_batch(Ebuf[:, 0, :])
                V.tensor_tensor(by_batch(is_v[:, :])[:, :, 0:S - 1], same[:, :, 0:S - 1], same[:, :, 1:S], ALU.mult).then_inc(mask_step, 1)
                dve.wait_ge(mask_step, 3)
                dve.wait_ge(mask_step, 3)
                V.tensor_scalar(is_l[:, :], is_v[:, :], -1.0, 1.0, ALU.mult, ALU.add).then_inc(masks_ready, 1)
                V.tensor_reduce(early[:, 0:1], by_batch(is_v[:, :])[:, :, 0:LATE], mybir.AxisListType.XY, ALU.add).then_inc(early_ready, 1)
                dve.wait_ge(early_ready, 1)
                V.tensor_copy(early[:, 1:2].bitcast(I32), early[:, 0:1]).then_inc(early_ready, 1)
                for i in range(2):
                    b = wait_full(dve, ("memN", i))
                    V.tensor_copy(memN[:, i, :, :], b[:, :].rearrange("p (r d) -> p r d", r=2)).then_inc(memN_ready, 1)
                    dve.wait_ge(memN_ready, i + 1)
                    dve.sem_inc(free(("memN", i)), 1)
                shift_unit(0, PAIRS)
                sum_unit(0, PAIRS)
                for m in range(DT):
                    dve.wait_ge(gate_ready, m + 1)
                    V.tensor_tensor(xn[:, m, :], xn[:, m, :], xv[:, m, :], ALU.mult).then_inc(gated, 1)
                    dve.wait_ge(gated, 2 * m + 1)
                    if m == 0:
                        dve.wait_ge(gate_ready, 2)
                    V.tensor_tensor(xT[:, m, :], xT[:, m, :], xn[:, m, :], ALU.add).then_inc(gated, 1)
                plain_norm(0, "L0_norm_w", xT, res_done)

                def layernorm(n, name):
                    b = wait_full(dve, ("mean", n))
                    for m in range(DT):
                        V.scalar_tensor_tensor(out=xn[:, m, :], in0=b[:, :], scalar=-1.0 / D, in1=xT[:, m, :],
                                               op0=ALU.mult, op1=ALU.add).then_inc(centred, 1)
                    dve.wait_ge(centred, 2 * n)
                    dve.sem_inc(free(("mean", n)), 1)
                    dve.wait_ge(rstd_ready, n + 1)
                    for m in range(DT):
                        V.scalar_tensor_tensor(out=xn[:, m, :], in0=xn[:, m, :], scalar=gain(name + "_g", m), in1=Ebuf[:, 2, :],
                                               op0=ALU.mult, op1=ALU.mult).then_inc(norm_step, 1)
                        dve.wait_ge(norm_step, 2 * (n - 1) + m + 1)
                        V.tensor_scalar(xn[:, m, :], xn[:, m, :], gain(name + "_b", m), None, ALU.add).then_inc(xn_ready, 1)

                layernorm(1, "L1_ln_q")
                dve.wait_ge(vbd_zeroed, 1)
                for j in range(JT + 1):
                    if j < JT:
                        b = wait_full(dve, ("l1v", j))
                        if j >= 2:
                            dve.wait_ge(pv_done, L1_U + j - 1)
                        for r in range(2):
                            for e in range(2):
                                src = b[64 * r:64 * r + 64, :].rearrange("p (c e d) -> p c e d", c=PAIRS, e=2)[:, :, e, :]
                                last = V.tensor_copy(l1_vbd[64 * e:64 * e + 64, j % 2, r:r + 2 * PAIRS - 1:2, 64 * e:64 * e + 64], src)
                        last.then_inc(l1_v_ready, 1)
                        dve.wait_ge(l1_v_ready, j + 1)
                        dve.sem_inc(free(("l1v", j)), 1)
                        shift_unit(L1_U + j, 8)
                    if j >= 1:
                        u, t = L1_U + j - 1, j - 1
                        dve.wait_ge(pv_done, u + 1)
                        if t >= 2:
                            dve.wait_ge(wo_done, t - 1)
                        V.tensor_copy(l1_att[:, t % 2, :], o_bank[:, :]).then_inc(o_taken, 1)
                    if j < JT:
                        sum_unit(L1_U + j, 8)

                def gated_residual(which, done, count):
                    dve.wait_ge(done, count)
                    for m in range(DT):
                        V.scalar_tensor_tensor(out=xT[:, m, :], in0=acc[m][:, :], scalar=gate_scalars[:, which:which + 1],
                                               in1=xT[:, m, :], op0=ALU.mult, op1=ALU.add).then_inc(res_done, 1)

                gated_residual(0, wo_done, JT)
                dve.wait_ge(res_done, 4)
                dve.sem_inc(acc_free, 1)
                layernorm(2, "L1_ln_ff")
                gated_residual(1, w2_done, L1_FF // P)
                dve.wait_ge(res_done, 6)
                dve.sem_inc(acc_free, 1)

                for n in (2, 3):
                    li = n - 2

                    def masked_norm(nn, name):
                        dve.wait_ge(rstd_ready, nn + 1)
                        V.tensor_tensor(Ebuf[:, 0, :], Ebuf[:, 2, :], is_l[:, :], ALU.mult).then_inc(norm_step, 1)
                        dve.wait_ge(norm_step, 4 + 2 * li + (nn - 3 * n + 3) // 2 + 1)
                        for m in range(DT):
                            V.scalar_tensor_tensor(out=xn[:, m, :], in0=xT[:, m, :], scalar=gain(name, m), in1=Ebuf[:, 0, :],
                                                   op0=ALU.mult, op1=ALU.mult).then_inc(xn_ready, 1)
                        dve.wait_ge(rstd_v_ready, 2 * li + (nn - 3 * n + 3) // 2 + 1)
                        for m in range(DT):
                            V.scalar_tensor_tensor(out=xv[:, m, :], in0=xT[:, m, :], scalar=gain(name, m), in1=Ebuf[:, 1, :],
                                                   op0=ALU.mult, op1=ALU.mult).then_inc(xv_ready, 1)

                    masked_norm(3 * n - 3, f"L{n}_ln_in_w")
                    for i in range(4):
                        b = wait_full(dve, ("rot", n, i))
                        V.tensor_tensor(by_batch(PT[:, i % 2, :]), by_batch(b[:, :]),
                                        cos_sin[:, 1, :].unsqueeze(1).broadcast_to([P, G, S]), ALU.mult).then_inc(sined, 1)
                        dve.wait_ge(sined, 4 * li + i + 1)
                        dve.sem_inc(free(("rot", n, i)), 1)
                        dve.wait_ge(cosined, 4 * li + i + 1)
                        V.tensor_tensor(qk[:, i, :], qk[:, i, :], PT[:, i % 2, :], ALU.add).then_inc(roped, 1)

                    def self_keys(i):
                        u, t, p = SELF_U(n) + i, i // PAIRS, i % PAIRS
                        dve.wait_ge(roped, 4 * li + 2 * t + 1)
                        if i >= 2:
                            dve.wait_ge(scores_ready, u - 1)
                        src = by_batch(qk[:, 2 * t, p * P:(p + 1) * P]).unsqueeze(2).broadcast_to([P, 2, 8, S])
                        rows = head_rows[:, 0, :].unsqueeze(1).unsqueeze(3).broadcast_to([P, 2, 8, S])
                        V.tensor_tensor(kbd[:, i % 2, :, :].rearrange("p r (h s) -> p r h s", h=8), src, rows, ALU.mult).then_inc(kbd_ready, 1)

                    def self_take(i):
                        u, t, p = SELF_U(n) + i, i // PAIRS, i % PAIRS
                        dve.wait_ge(pv_done, u + 1)
                        at = slice(p * P, (p + 1) * P)
                        V.tensor_tensor(xn[:, t, at], o_bank[:, 0:P], is_l[:, at], ALU.mult)
                        V.tensor_tensor(xv[:, t, at], o_bank[:, 0:P], is_v[:, at], ALU.mult).then_inc(o_taken, 1)

                    self_keys(0)
                    dve.wait_ge(v_ready, 2 * li + 2)
                    for i in range(8 + 3):
                        if i + 1 < 8:
                            self_keys(i + 1)
                        if i < 8:
                            shift_unit(SELF_U(n) + i, 8)
                        if 1 <= i < 9:
                            sum_unit(SELF_U(n) + i - 1, 8)
                        if i >= 3:
                            self_take(i - 3)
                    for m in range(DT):
                        residual(("dense", n, m), m)
                        dve.wait_ge(res_done, 6 * li + 6 + m + 1)
                        dve.sem_inc(free(("dense", n, m)), 1)
                    plain_norm(3 * n - 2, f"L{n}_ln_post_cross_w", xn, xn_ready)

                    def cross_keys(p):
                        if p == 0:
                            dve.wait_ge(ck_ready, li + 1)
                        if p >= 2:
                            dve.wait_ge(scores_ready, CROSS_U(n) + 2 * p - 2)
                        src = by_batch(qk[:, 1, p * P:(p + 1) * P]).unsqueeze(2).broadcast_to([P, 2, 8, S])
                        rows = head_rows[:, 1, :].unsqueeze(1).unsqueeze(3).broadcast_to([P, 2, 8, S])
                        V.tensor_tensor(kbd[:, p % 2, :, :].rearrange("p r (h s) -> p r h s", h=8), src, rows, ALU.mult).then_inc(kbd_ready, 1)

                    def cross_take(i):
                        u, p, r8 = CROSS_U(n) + i, i // 2, i % 2
                        dve.wait_ge(pv_done, u + 1)
                        V.tensor_copy(xv[64 * r8:64 * r8 + 64, 0, p * P:(p + 1) * P], o_bank[64 * r8:64 * r8 + 64, 0:P]).then_inc(o_taken, 1)

                    cross_keys(0)
                    for i in range(8 + 3):
                        if i % 2 == 0 and i // 2 + 1 < PAIRS:
                            cross_keys(i // 2 + 1)
                        if i < 8:
                            shift_unit(CROSS_U(n) + i, 8)
                        if 1 <= i < 9:
                            sum_unit(CROSS_U(n) + i - 1, 8)
                        if i >= 3:
                            cross_take(i - 3)
                    for m in range(DT):
                        residual(("cdense", n, m), m)
                        dve.wait_ge(res_done, 6 * li + 8 + m + 1)
                        dve.sem_inc(free(("cdense", n, m)), 1)
                    masked_norm(3 * n - 1, f"L{n}_ln_post_attn_w")
                    for j in range(FT):
                        rows = P if j < FT - 1 else FR
                        b = wait_full(dve, ("u", n, j))
                        dve.wait_ge(silu_ready, FT * li + j + 1)
                        V.tensor_tensor(silu_g[0:rows, j % 2, :], silu_g[0:rows, j % 2, :], b[0:rows, :], ALU.mult).then_inc(h_ready, 1)
                        dve.wait_ge(h_ready, FT * li + j + 1)
                        dve.sem_inc(free(("u", n, j)), 1)
                    dve.wait_ge(down_done, FT * (li + 1))
                    for m in range(DT):
                        V.tensor_tensor(xT[:, m, :], acc[m][:, :], xT[:, m, :], ALU.add).then_inc(res_done, 1)
                    dve.wait_ge(res_done, 6 * li + 12)
                    dve.sem_inc(acc_free, 1)

            @block.gpsimd
            def _(pool):
                G_ = nc.gpsimd

                def prob_unit(u, g):
                    pool.wait_ge(rcp_ready, u + 1)
                    v = Ebuf[:, u % 3, 0:g * S].rearrange("p (g s) -> p g s", s=S)
                    G_.tensor_tensor(v, v, row_rcp[:, u % 3, 0:g].unsqueeze(2).broadcast_to([P, g, S]), ALU.mult).then_inc(probs_ready, 1)

                G_.memset(arena[:, A_K:A_K + 2048], 0.0).then_inc(kbd_zeroed, 1)
                prob_unit(0, PAIRS)
                pool.wait_ge(pv_done, 1)
                G_.memset(arena[:, A_QK:A_QK + 2048], 0.0).then_inc(vbd_zeroed, 1)
                for j in range(JT):
                    prob_unit(L1_U + j, 8)
                pool.wait_ge(wo_done, JT)
                G_.memset(arena[:, A_VS:A_VS + 3072], 0.0).then_inc(v_zeroed, 1)
                pool.wait_ge(masks_ready, 1)
                for n in (2, 3):
                    li = n - 2

                    def late_rstd(nn):
                        pool.wait_ge(rstd_ready, nn + 1)
                        G_.tensor_tensor(Ebuf[:, 1, :], Ebuf[:, 2, :], is_v[:, :], ALU.mult).then_inc(rstd_v_ready, 1)

                    late_rstd(3 * n - 3)
                    for i in range(4):
                        pool.wait_ge(full(("rot", n, i)), PROJ["rot", n, i] // 2 + 1)
                        v = by_batch(qk[:, i, :])
                        G_.tensor_tensor(v, v, cos_sin[:, 0, :].unsqueeze(1).broadcast_to([P, G, S]), ALU.mult).then_inc(cosined, 1)
                    for i in range(8):
                        prob_unit(SELF_U(n) + i, 8)
                    for i in range(8):
                        prob_unit(CROSS_U(n) + i, 8)
                    late_rstd(3 * n - 1)
                    for j in range(FT):
                        rows = P if j < FT - 1 else FR
                        pool.wait_ge(h_ready, FT * li + j + 1)
                        if j >= 2:
                            pool.wait_ge(down_done, FT * li + j - 1)
                        G_.tensor_tensor(hid_l[j % 2][0:rows, :], silu_g[0:rows, j % 2, :], is_l[0:rows, :], ALU.mult).then_inc(hl_ready, 1)
                        G_.tensor_tensor(hid_v[0:rows, j % 2, :], silu_g[0:rows, j % 2, :], is_v[0:rows, :], ALU.mult).then_inc(hv_ready, 1)

        nums = [s.num for s in sems]
        assert nums == list(range(nums[0], nums[0] + len(nums)))
        nc.sync.sem_clear(range(nums[0], nums[-1] + 1))
        nc.all_engine_barrier()
    ctx.close()


def kernel(**inputs):
    import concourse.bacc as _bacc
    from concourse.bass_utils import run_bass_kernel_spmd as _run

    nc = _bacc.Bacc("TRN2", target_bir_lowering=False, num_devices=1)
    rows = {"x": np.asarray(inputs["x"]).reshape(B * S, D), "ctx": np.asarray(inputs["ctx_1024"]).reshape(B * S, E),
            "types": np.asarray(inputs["mask_BxS_ik0"]).reshape(B * S), "positions": np.asarray(inputs["pos_1xS"]),
            "media_mask": np.ascontiguousarray(inputs["mask_BxS2_bk0"]).view(np.int32),
            "L0_W_memT": np.asarray(inputs["L0_xattn_W_mem"]).T, "L0_W_gateT": np.asarray(inputs["L0_xattn_W_gate"]).T}
    for name, v in inputs.items():
        if "_xattn_" in name and name not in ("L0_xattn_W_mem", "L0_xattn_W_gate"):
            rows[name.replace("_xattn_", "_")] = np.asarray(v)
    rows["c_ident"] = np.eye(P, dtype=np.float32)
    half = HD // 2
    turn = np.zeros((P, P), np.float32)
    for j in range(P):
        turn[j + half if j % HD < half else j - half, j] = -1.0 if j % HD < half else 1.0
    rows["c_rotate"] = turn
    lane = np.arange(P)
    rows["c_head_rows"] = np.stack([lane[:, None] // HD == np.arange(8), (lane[:, None] % 64) // CHD == np.arange(8)], 1).astype(np.float32)
    rows["c_causal"] = np.where(np.arange(S)[None, :] <= (lane % S)[:, None], 0.0, NEG).astype(np.float32)
    inv = (1.0 / np.float32(10000.0) ** (np.arange(0, HD, 2, dtype=np.float32) / np.float32(HD))).astype(np.float32)
    angle = np.outer(np.arange(S, dtype=np.float32), inv)[:, (lane % HD) % half]
    rows["c_cos_sin"] = np.concatenate([np.cos(angle), np.sin(angle)], 1).astype(np.float32)
    rows["c_index"] = np.arange(S, dtype=np.float32)[:, None]
    rows["c_parity"] = (lane[None, :] // 64 == np.arange(2)[:, None]).astype(np.float32)
    arrays, args = {}, {}
    for name, v in rows.items():
        arrays[f"in_{name}"] = np.ascontiguousarray(v)
        args[name] = nc.dram_tensor(f"in_{name}", v.shape, mybir.dt.from_np(v.dtype), kind="ExternalInput").ap()
    out = nc.dram_tensor("out_x", (B * S, D), F32, kind="ExternalOutput").ap()
    xattn_kernel(nc, args, out)
    r = _run(nc, [arrays], core_ids=[0])
    return r.results[0]["out_x"].reshape(B, S, D)
```

```python
from contextlib import ExitStack

import numpy as np
import concourse.bass as bass
from concourse import mybir

ALU = mybir.AluOpType
ACT = mybir.ActivationFunctionType
F32 = mybir.dt.float32
BF16 = mybir.dt.bfloat16
I32 = mybir.dt.int32
U8 = mybir.dt.uint8
AX_X = mybir.AxisListType.X

P = 128
B, S, D, E = 64, 64, 256, 128
G = 8
GROUPS = B // G
T = G * S
PAIRS = G // 2
DT = D // P
H = 16
L1_HD, L1_INNER, L1_FF = 64, 1024, 1024
JT = L1_INNER // P
HD, CHD = D // H, E // H
FF = 688
FT = -(-FF // P)
FR = FF - (FT - 1) * P
LATE = 48
NEG = -3.3e38
EPS_RMS, EPS_LN = 1e-6, 1e-5

GAINS = ["L0_norm_w", "L0_b_gate", "L1_ln_q_g", "L1_ln_q_b", "L1_ln_ff_g", "L1_ln_ff_b",
         "L2_ln_in_w", "L2_ln_post_cross_w", "L2_ln_post_attn_w",
         "L3_ln_in_w", "L3_ln_post_cross_w", "L3_ln_post_attn_w"]



def projection_order():
    uses = [("in", "x", 0), ("in", "x", 1), ("in", "ctx"), ("mem", 0), ("mem", 1), ("memN", 0), ("memN", 1),
            ("gate", 0), ("gate", 1), ("norm", 0)]
    uses += [("mean", 1), ("norm", 1)]
    for j in range(JT):
        uses += [("l1k", j), ("l1v", j), ("l1q", j)]
    uses += [("mean", 2), ("norm", 2)] + [("l1h", j) for j in range(L1_FF // P)]
    for layer in (2, 3):
        n = 3 * layer - 3
        uses += [("norm", n)]
        uses += [("qk", layer, i) for i in range(4)] + [("rot", layer, i) for i in range(4)]
        uses += [("v", layer, i) for i in range(2)] + [("dense", layer, m) for m in range(DT)]
        uses += [("ck", layer), ("norm", n + 1), ("cv", layer), ("cq", layer)]
        uses += [("cdense", layer, m) for m in range(DT)] + [("norm", n + 2)]
        for j in range(FT):
            uses += [("g", layer, j), ("u", layer, j)]
    uses += [("out", 0), ("out", 1)]
    return {key: n for n, key in enumerate(uses)}


PROJ = projection_order()
L1_U = 1


def SELF_U(layer):
    return 1 + JT + 16 * (layer - 2)


def CROSS_U(layer):
    return SELF_U(layer) + 8


def xattn_kernel(nc, a, out):
    ctx = ExitStack()

    def sb(name, shape, dt=F32):
        return ctx.enter_context(nc.sbuf_tensor(name, shape, dt))

    def pb(name):
        return ctx.enter_context(nc.psum_tensor(name, [P, T], F32))

    sems = []

    def sem(name):
        s = ctx.enter_context(nc.semaphore(name))
        return s

    def turn_sem(name):
        s = sem(name)
        sems.append(s)
        return s

    w_mem = sb("w_mem", [P, D])
    w_gate = sb("w_gate", [P, 2 * DT, D])
    w_q = sb("w_q", [P, DT, L1_INNER])
    w_kv = sb("w_kv", [P, 2 * L1_INNER])
    w_o = sb("w_o", [P, JT, D])
    w_1 = sb("w_1", [P, DT, L1_FF])
    w_2 = sb("w_2", [P, L1_FF // P, D])
    w_qkv, w_dense, w_cq, w_ckv, w_cdense, w_g, w_u, w_down = ({} for _ in range(8))
    for n in (2, 3):
        w_cq[n] = sb(f"w{n}_cq", [P, DT, E])
        w_ckv[n] = sb(f"w{n}_ckv", [P, 2 * E])
        w_cdense[n] = sb(f"w{n}_cdense", [P, D])
        for e in "lv":
            w_qkv[n, e] = sb(f"w{n}_{e}_qkv", [P, DT, 3 * D])
            w_dense[n, e] = sb(f"w{n}_{e}_dense", [P, DT, D])
            w_g[n, e] = sb(f"w{n}_{e}_gate", [P, DT, FF])
            w_u[n, e] = sb(f"w{n}_{e}_up", [P, DT, FF])
            w_down[n, e] = sb(f"w{n}_{e}_down", [P, FT, D])
    gains = sb("gains", [P, len(GAINS), DT])
    small = sb("small", [P, 8])
    gate_scalars = small[:, 0:2]
    norm_consts = small[:, 4:7]
    warm = small[:, 7:8]
    ident = sb("ident", [P, P])
    rotate = sb("rotate", [P, P])
    ones = sb("ones", [P, P])
    cos_sin = sb("cos_sin", [P, 2, S])
    head_rows = sb("head_rows", [P, 2, 8], BF16)
    self_sum = sb("self_sum", [P, 32])
    cross_sum = sb("cross_sum", [P, 48])
    ident_bf = sb("ident_bf", [P, P], BF16)
    causal_bf = sb("causal_bf", [P, S], BF16)
    parity_bf = sb("parity_bf", [2, P], BF16)

    xT = sb("xT", [P, DT, T])
    ctxT = sb("ctxT", [P, T])
    xn = sb("xn", [P, DT, T])
    xv = sb("xv", [P, DT, T])
    is_v = sb("is_v", [P, T], BF16)
    is_l = sb("is_l", [P, T], BF16)
    early = small[:, 2:4]
    media = sb("media", [P, PAIRS * S // 2])
    media_bias = media[0:2, :].bitcast(BF16).rearrange("p (a s) -> p a s", s=S)
    media_words = media[64:66, 0:PAIRS * S // 4].bitcast(I32)
    media_raw = media[64:66, 0:PAIRS * S // 4].bitcast(U8).rearrange("p (a s) -> p a s", s=S)
    Ebuf = sb("Ebuf", [P, 3, T])
    PT = sb("PT", [P, 2, T])
    row_max = sb("row_max", [P, 2, 8])
    row_sum = sb("row_sum", [P, 8])
    rms_cols, rstd = row_sum[:, 0:PAIRS], row_sum[:, PAIRS:2 * PAIRS]
    row_rcp = sb("row_rcp", [P, 3, 8])
    arena = sb("arena", [P, 7168])
    A_K, A_VS, A_VC, A_QK = 0, 2048, 4096, 5120

    def part(at, *shape):
        n = int(np.prod(shape))
        v = arena[:, at:at + n]
        if len(shape) == 2:
            v = v.rearrange("p (a b) -> p a b", a=shape[0])
        if len(shape) == 3:
            v = v.rearrange("p (a b c) -> p a b c", a=shape[0], b=shape[1])
        if len(shape) == 4:
            v = v.rearrange("p (a b c d) -> p a b c d", a=shape[0], b=shape[1], c=shape[2])
        return v

    x_raw = part(A_VS, PAIRS, D)
    ctx_raw = part(A_VS + 1024, PAIRS, E)
    tt_raw = arena[:, A_VS + 1536:A_VS + 2048].bitcast(I32)
    memT = part(A_QK, DT, T)
    memN = part(A_QK + 1024, 2, 2, D)
    l1_kbd = part(A_K, 2, G, P)
    l1_vbd = part(A_QK, 2, G, P)
    l1_q = part(A_VS, 2, T)
    l1_att = part(A_VS + 1024, 2, T)
    l1_hid = part(A_K, 3, T)
    kbd = part(A_K, 2, 2, 8 * S)
    v_self = part(A_VS, G, 8, 32)
    v_cross = part(A_VC, 2, 2, 8, 32)
    qk = part(A_QK, 4, T)
    silu_g = part(A_K, 2, T)
    hid_l0 = part(A_K + 1024, 2, T)
    hid_v = part(A_QK, 2, T)
    hid_l = [hid_l0[:, 0, :], hid_l0[:, 1, :]]
    out_rows = PT[:, :, :].rearrange("p a t -> p (a t)").rearrange("p (q d) -> p q d", d=D)

    proj_bank = [pb("proj0"), pb("proj1")]
    score_bank = [pb("scores0"), pb("scores1")]
    pt_bank = pb("pt_bank")
    o_bank = pb("o_bank")
    acc = [pb("acc0"), pb("acc1")]

    s_const = sem("s_const")
    s_setup = sem("s_setup")
    s_table = sem("s_table")
    w_loaded = {k: sem(f"w_{k}_loaded") for k in (0, 1, 2, 3)}
    s_first = sem("s_first")

    proj_full = [turn_sem(f"proj{i}_full") for i in range(2)]
    proj_free = [turn_sem(f"proj{i}_free") for i in range(2)]
    acc_full = turn_sem("acc_full")
    acc_free = turn_sem("acc_free")
    scores_ready = turn_sem("scores_ready")
    maxed = turn_sem("maxed")
    shifted = turn_sem("shifted")
    exped = turn_sem("exped")
    summed = turn_sem("summed")
    rcp_ready = turn_sem("rcp_ready")
    probs_ready = turn_sem("probs_ready")
    pt_full = turn_sem("pt_full")
    pt_ready = turn_sem("pt_ready")
    pv_done = turn_sem("pv_done")
    o_taken = turn_sem("o_taken")
    xT_loaded = turn_sem("xT_loaded")
    masks_ready = turn_sem("masks_ready")
    mask_step = turn_sem("mask_step")
    early_ready = turn_sem("early_ready")
    bias_ready = turn_sem("bias_ready")
    mem_ready = turn_sem("mem_ready")
    memN_ready = turn_sem("memN_ready")
    l0_half = turn_sem("l0_half")
    l0_ctx_ready = turn_sem("l0_ctx_ready")
    gate_ready = turn_sem("gate_ready")
    gated = turn_sem("gated")
    kbd_zeroed = turn_sem("kbd_zeroed")
    vbd_zeroed = turn_sem("vbd_zeroed")
    v_zeroed = turn_sem("v_zeroed")
    res_done = turn_sem("res_done")
    centred = turn_sem("centred")
    sq_ready = turn_sem("sq_ready")
    ln_step = turn_sem("ln_step")
    sums_ready = turn_sem("sums_ready")
    rstd_ready = turn_sem("rstd_ready")
    rms_ready = turn_sem("rms_ready")
    norm_step = turn_sem("norm_step")
    table_loaded = turn_sem("table_loaded")
    gained = turn_sem("gained")
    pre_step = turn_sem("pre_step")
    inverted = turn_sem("inverted")
    att_split = turn_sem("att_split")
    att_ready = turn_sem("att_ready")
    cv_ready = turn_sem("cv_ready")
    xn_ready = turn_sem("xn_ready")
    xv_ready = turn_sem("xv_ready")
    l1_k_ready = turn_sem("l1_k_ready")
    l1_q_ready = turn_sem("l1_q_ready")
    l1_v_ready = turn_sem("l1_v_ready")
    wo_done = turn_sem("wo_done")
    hid_ready = turn_sem("hid_ready")
    w2_done = turn_sem("w2_done")
    qk_ready = turn_sem("qk_ready")
    cosined = turn_sem("cosined")
    sined = turn_sem("sined")
    roped = turn_sem("roped")
    v_ready = turn_sem("v_ready")
    kbd_ready = [turn_sem(f"kbd{r}_ready") for r in range(2)]
    cq_ready = turn_sem("cq_ready")
    ck_ready = turn_sem("ck_ready")
    vc_ready = turn_sem("vc_ready")
    silu_ready = turn_sem("silu_ready")
    h_ready = turn_sem("h_ready")
    hl_ready = turn_sem("hl_ready")
    hv_ready = turn_sem("hv_ready")
    down_done = turn_sem("down_done")
    out_ready = turn_sem("out_ready")
    stored = turn_sem("stored")
    next_loaded = turn_sem("next_loaded")

    def bank(key):
        return proj_bank[PROJ[key] % 2]

    def fill(pe, key):
        n = PROJ[key]
        if n >= 2:
            pe.wait_ge(proj_free[n % 2], n // 2)
        return proj_bank[n % 2]

    def full(key):
        return proj_full[PROJ[key] % 2]

    def free(key):
        return proj_free[PROJ[key] % 2]

    def wait_full(eng, key):
        n = PROJ[key]
        eng.wait_ge(proj_full[n % 2], n // 2 + 1)
        return proj_bank[n % 2]

    def gain(name, m):
        return gains[:, GAINS.index(name), m:m + 1]

    def by_batch(v):
        return v.rearrange("p (b s) -> p b s", s=S)

    def key_blocks(kind, tile, p, r, slot):
        return (kbd[:, slot, r, :].rearrange("p (h s) -> p h s", h=8),
                qk[:, tile, p * P + r * S:p * P + (r + 1) * S].unsqueeze(1).broadcast_to([P, 8, S]),
                head_rows[:, kind, :].unsqueeze(2).broadcast_to([P, 8, S]))

    def load_group(q, i, done):
        rows = a["x"].rearrange("(g t p) d -> g p t d", g=GROUPS, p=P)[i]
        q.dma_start(x_raw, rows).then_inc(done, 16)
        rows = a["ctx"].rearrange("(g t p) d -> g p t d", g=GROUPS, p=P)[i]
        q.dma_start(ctx_raw, rows).then_inc(done, 16)
        q.dma_start(tt_raw, a["types"].rearrange("(g o t) -> g o t", g=GROUPS, o=1)[i].broadcast_to([P, T])).then_inc(done, 16)
        q.dma_start(media_words.rearrange("p (a s) -> p a s", a=PAIRS), a["media_mask"].rearrange("(g b r) s -> g r b s", g=GROUPS, r=2)[i]).then_inc(done, 16)

    with nc.Block() as block:
        @block.sync
        def _(q):
            load_group(q, 0, s_first)
            q.dma_start(ident[:, :], a["c_ident"]).then_inc(s_const, 16)
            q.dma_start(rotate[:, :], a["c_rotate"]).then_inc(s_const, 16)
            q.dma_start(Ebuf[:, 0, 64:80], a["c_head_rows"]).then_inc(s_const, 16)
            q.dma_start(self_sum[:, :], a["c_self_sum"]).then_inc(s_const, 16)
            q.dma_start(cross_sum[:, :], a["c_cross_sum"]).then_inc(s_const, 16)
            q.dma_start(Ebuf[:, 0, 0:S], a["c_causal"]).then_inc(s_const, 16)
            q.dma_start(Ebuf[0:S, 1, 0:2 * P], a["c_cos_sin"]).then_inc(s_const, 16)
            q.dma_start(Ebuf[0:S, 2, 0:S].bitcast(I32), a["positions"].broadcast_to([S, S])).then_inc(s_const, 16)
            q.dma_start(Ebuf[0:S, 2, S:S + 1], a["c_index"]).then_inc(s_const, 16)
            q.dma_start(Ebuf[0:2, 2, 128:256], a["c_parity"]).then_inc(s_const, 16)
            q.dma_start(gate_scalars[:, 0:1], a["L1_attn_gate"].rearrange("(o n) -> o n", o=1).broadcast_to([P, 1])).then_inc(s_const, 16)
            q.dma_start(gate_scalars[:, 1:2], a["L1_ff_gate"].rearrange("(o n) -> o n", o=1).broadcast_to([P, 1])).then_inc(s_const, 16)
            for n, name in enumerate(GAINS):
                with nc.allow_non_contiguous_dma(reason="one word per row, once"):
                    q.dma_start(gains[:, n, :], a[name].rearrange("(m p) -> p m", p=P)).then_inc(s_const, 16)

            def load_w(dst, src, k):
                q.dma_start(dst, src).then_inc(w_loaded[k], 16)

            def tiles(v):
                return v.rearrange("(t p) n -> p t n", p=P)

            load_w(w_mem[:, :], a["L0_W_memT"], 0)
            load_w(w_gate[:, :, :], tiles(a["L0_W_gateT"]), 0)
            load_w(w_kv[:, :], a["L1_Wkv"], 1)
            load_w(w_q[:, :, :], tiles(a["L1_Wq"]), 1)
            load_w(w_o[:, :, :], tiles(a["L1_Wo"]), 1)
            load_w(w_1[:, :, :], tiles(a["L1_W1"]), 1)
            load_w(w_2[:, :, :], tiles(a["L1_W2"]), 1)
            for n in (2, 3):
                for e in "lv":
                    load_w(w_qkv[n, e][:, :, :], tiles(a[f"L{n}_{e}_qkv"]), n)
                    load_w(w_dense[n, e][:, :, :], tiles(a[f"L{n}_{e}_dense"]), n)
                load_w(w_cq[n][:, :, :], tiles(a[f"L{n}_cq_w"]), n)
                load_w(w_ckv[n][:, :], a[f"L{n}_ckv_w"], n)
                load_w(w_cdense[n][:, :], a[f"L{n}_cdense_w"], n)
                for e in "lv":
                    load_w(w_g[n, e][:, :, :], tiles(a[f"L{n}_{e}_gate"]), n)
                    load_w(w_u[n, e][:, :, :], tiles(a[f"L{n}_{e}_up"]), n)
                    down = a[f"L{n}_{e}_down"]
                    load_w(w_down[n, e][:, 0:FT - 1, :], tiles(down[0:(FT - 1) * P, :]), n)
                    load_w(w_down[n, e][0:FR, FT - 1, :], down[(FT - 1) * P:FF, :], n)

        @block.vector
        def _(dve):
            nc.vector.memset(ones[:, :], 1.0).then_inc(s_setup, 1)
            nc.vector.memset(norm_consts[:, 0:1], EPS_RMS).then_inc(s_setup, 1)
            nc.vector.memset(norm_consts[:, 1:2], EPS_LN).then_inc(s_setup, 1)
            nc.vector.memset(norm_consts[:, 2:3], 0.0).then_inc(s_setup, 1)
            dve.wait_ge(s_const, 16 * (12 + len(GAINS)))
            nc.vector.tensor_copy(ident_bf[:, :], ident[:, :]).then_inc(s_setup, 1)
            nc.vector.tensor_copy(causal_bf[:, :], Ebuf[:, 0, 0:S]).then_inc(s_setup, 1)
            nc.vector.tensor_copy(parity_bf[:, :], Ebuf[0:2, 2, 128:256]).then_inc(s_setup, 1)
            nc.vector.tensor_copy(head_rows[:, :, :], Ebuf[:, 0, 64:80].rearrange("p (a h) -> p a h", a=2)).then_inc(s_setup, 1)
            pos, wrap, hot = Ebuf[0:S, 2, 256:256 + S], Ebuf[0:S, 2, 320:320 + S], Ebuf[0:S, 2, 384:384 + S]
            nc.vector.tensor_copy(pos, Ebuf[0:S, 2, 0:S].bitcast(I32)).then_inc(s_table, 1)
            dve.wait_ge(s_table, 1)
            nc.vector.tensor_scalar(wrap, pos, 0.0, float(S), ALU.is_lt, ALU.mult).then_inc(s_table, 1)
            dve.wait_ge(s_table, 2)
            nc.vector.tensor_tensor(pos, pos, wrap, ALU.add).then_inc(s_table, 1)
            dve.wait_ge(s_table, 3)
            nc.vector.tensor_scalar(wrap, pos, 0.0, float(S - 1), ALU.max, ALU.min).then_inc(s_table, 1)
            dve.wait_ge(s_table, 4)
            nc.vector.tensor_scalar(hot, wrap, Ebuf[0:S, 2, S:S + 1], None, ALU.is_equal).then_inc(s_table, 1)
            dve.wait_ge(s_table, 6)
            nc.vector.tensor_copy(cos_sin[:, :, :], proj_bank[0][:, 0:2 * S].rearrange("p (a s) -> p a s", a=2)).then_inc(s_table, 1)
            dve.wait_ge(s_table, 7)
            dve.wait_ge(s_first, 64)

        @block.tensor
        def _(pe):
            pe.wait_ge(s_table, 5)
            for n in range(2):
                last = nc.tensor.matmul(proj_bank[0][:, n * S:(n + 1) * S], Ebuf[0:S, 1, n * P:(n + 1) * P],
                                        Ebuf[0:S, 2, 384:384 + S], start=True, stop=True)
            last.then_inc(s_table, 1)

        @block.scalar
        def _(act):
            act.wait_ge(s_const, 16 * (12 + len(GAINS)))
            nc.scalar.activation(gate_scalars[:, :], gate_scalars[:, :], ACT.Tanh).then_inc(s_setup, 1)

        @block.gpsimd
        def _(pool):
            pool.wait_ge(s_setup, 9)

    with nc.Fori(0, GROUPS) as turn:
        with nc.Block() as block:
            @block.sync
            def _(q):
                q.wait_ge(pv_done, SELF_U(3) + 8)
                load_group(q, (turn + 1) % GROUPS, next_loaded)
                q.wait_ge(out_ready, 2)
                q.dma_start(out.rearrange("(g t p) d -> g p t d", g=GROUPS, p=P)[turn], out_rows).then_inc(stored, 16)
                q.wait_ge(stored, 16)
                q.wait_ge(next_loaded, 64)

            @block.tensor
            def _(pe):
                mm = nc.tensor.matmul

                def transposes_unit(u, cols):
                    if u < SELF_U(2):
                        pe.wait_ge(probs_ready, u + 1)
                    else:
                        pe.wait_ge(exped, u + 1)
                    if u >= 1:
                        pe.wait_ge(pt_ready, u)
                    for c in range(cols // P):
                        last = nc.tensor.transpose(pt_bank[:, c * P:(c + 1) * P], Ebuf[:, u % 3, c * P:(c + 1) * P], ident[:, :])
                    last.then_inc(pt_full, 1)

                def keep_busy(times):
                    for _ in range(times):
                        mm(score_bank[0][:, :].rearrange("p (h s) -> p h s", h=8), ident_bf[:, :],
                           causal_bf[:, :].unsqueeze(1).broadcast_to([P, 8, S]), start=True, stop=True)

                def norm_sums(n, src_ready, count):
                    b = fill(pe, ("norm", n))
                    keep_busy(6)
                    for m in range(DT):
                        pe.wait_ge(src_ready, count - DT + m + 1)
                        for t in range(PAIRS):
                            last = mm(b[:, t:t + 1], Ebuf[:, m, t * P:(t + 1) * P], ones[:, 0:1], start=(m == 0 and t == 0),
                                      stop=(m == DT - 1), skip_group_check=True)
                    last.then_inc(sums_ready, 1)

                def norm_spread(n):
                    b = bank(("norm", n))
                    keep_busy(3)
                    pe.wait_ge(rstd_ready, n + 1)
                    for t in range(PAIRS):
                        last = mm(b[:, t * P:(t + 1) * P], rstd[:, t:t + 1].broadcast_to([P, P]), ident[:, :], start=True, stop=True)
                    last.then_inc(full(("norm", n)), 1)
                    keep_busy(3)

                def mean_sums(n):
                    b = fill(pe, ("mean", n))
                    keep_busy(6)
                    pe.wait_ge(res_done, 2 * n)
                    for m in range(DT):
                        last = mm(b[:, :], ones[:, :], xT[:, m, :], start=(m == 0), stop=(m == DT - 1))
                    last.then_inc(full(("mean", n)), 1)

                for m in range(DT):
                    b = fill(pe, ("in", "x", m))
                    for t in range(PAIRS):
                        last = nc.tensor.transpose(b[:, t * P:(t + 1) * P], x_raw[:, t, m * P:(m + 1) * P], ident[:, :])
                    last.then_inc(full(("in", "x", m)), 1)
                b = fill(pe, ("in", "ctx"))
                for t in range(PAIRS):
                    last = nc.tensor.transpose(b[:, t * P:(t + 1) * P], ctx_raw[:, t, :], ident[:, :])
                last.then_inc(full(("in", "ctx")), 1)

                pe.wait_ge(w_loaded[0], 32)
                pe.wait_ge(xT_loaded, 3)
                for m in range(DT):
                    b = fill(pe, ("mem", m))
                    mm(b[:, :], w_mem[:, m * P:(m + 1) * P], ctxT[:, :], start=True, stop=True).then_inc(full(("mem", m)), 1)
                for i in range(2):
                    b = fill(pe, ("memN", i))
                    for r in range(2):
                        for e in range(2):
                            n = 2 * (2 * i + e) + r
                            last = mm(b[64 * e:64 * e + 64, r * D:(r + 1) * D], ctxT[:, n * S:(n + 1) * S], w_mem[:, :],
                                      start=True, stop=True)
                    last.then_inc(full(("memN", i)), 1)
                pe.wait_ge(mem_ready, DT)
                for p in range(PAIRS):
                    for r in range(2):
                        n = 2 * p + r
                        for m in range(DT):
                            last = mm(score_bank[0][64 * r:64 * r + 64, p * S:(p + 1) * S], xT[:, m, n * S:(n + 1) * S],
                                      memT[:, m, n * S:(n + 1) * S], start=(m == 0), stop=(m == DT - 1))
                last.then_inc(scores_ready, 1)
                transposes_unit(0, PAIRS * S)
                pe.wait_ge(pt_ready, 1)
                pe.wait_ge(memN_ready, 2)
                for e in range(2):
                    for m in range(DT):
                        for i in range(2):
                            for r in range(2):
                                n, at = 2 * (2 * i + e) + r, i * P + r * S
                                last = mm(acc[m][:, n * S:(n + 1) * S], memN[64 * e:64 * e + 64, i, r, m * P:(m + 1) * P],
                                          PT[64 * e:64 * e + 64, 0, at:at + S], start=True, stop=True)
                    if e == 0:
                        last.then_inc(l0_half, 1)
                        pe.wait_ge(l0_half, 1)
                last.then_inc(pv_done, 1)
                for m in range(DT):
                    b = fill(pe, ("gate", m))
                    for k in range(DT):
                        mm(b[:, :], w_gate[:, k, m * P:(m + 1) * P], xT[:, k, :], start=(k == 0), stop=False)
                    for k in range(DT):
                        pe.wait_ge(l0_ctx_ready, k + 1)
                        last = mm(b[:, :], w_gate[:, DT + k, m * P:(m + 1) * P], xv[:, k, :], start=False, stop=(k == DT - 1))
                    last.then_inc(full(("gate", m)), 1)
                norm_sums(0, sq_ready, 2)
                norm_spread(0)

                mean_sums(1)
                norm_sums(1, sq_ready, 4)
                norm_spread(1)
                pe.wait_ge(w_loaded[1], 16 * 5)
                pe.wait_ge(bias_ready, 1)
                for j in range(JT + 2):
                    if j < JT:
                        b = fill(pe, ("l1k", j))
                        mm(b[:, :], w_kv[:, j * P:(j + 1) * P], ctxT[:, :], start=True, stop=True).then_inc(full(("l1k", j)), 1)
                        b = fill(pe, ("l1v", j))
                        for p in range(PAIRS):
                            last = mm(b[:, p * P:(p + 1) * P], ctxT[:, p * P:(p + 1) * P],
                                      w_kv[:, L1_INNER + j * P:L1_INNER + (j + 1) * P], start=True, stop=True)
                        last.then_inc(full(("l1v", j)), 1)
                        b = fill(pe, ("l1q", j))
                        for k in range(DT):
                            if j == 0:
                                pe.wait_ge(xn_ready, k + 1)
                            last = mm(b[:, :], w_q[:, k, j * P:(j + 1) * P], xn[:, k, :], start=(k == 0), stop=(k == DT - 1))
                        last.then_inc(full(("l1q", j)), 1)
                    if 1 <= j <= JT:
                        transposes_unit(L1_U + j - 1, T)
                    if j < JT:
                        u = L1_U + j
                        pe.wait_ge(shifted, u - 1)
                        pe.wait_ge(l1_k_ready, j + 1)
                        pe.wait_ge(l1_q_ready, j + 1)
                        sc = score_bank[u % 2]
                        mm(sc[:, :].rearrange("p (b h s) -> p b h s", b=PAIRS, h=2), parity_bf[:, :],
                           media_bias.unsqueeze(2).broadcast_to([2, PAIRS, 2, S]), start=True, stop=True)
                        for p in range(PAIRS):
                            for r in range(2):
                                n = 2 * p + r
                                last = mm(sc[64 * r:64 * r + 64, p * P:(p + 1) * P], l1_q[:, j % 2, n * S:(n + 1) * S],
                                          l1_kbd[:, j % 2, n, :], start=False, stop=True, skip_group_check=True)
                        last.then_inc(scores_ready, 1)
                    if 1 <= j <= JT:
                        u = L1_U + j - 1
                        pe.wait_ge(pt_ready, u + 1)
                        pe.wait_ge(l1_v_ready, j)
                        pe.wait_ge(o_taken, u)
                        for n in range(G):
                            last = mm(o_bank[:, n * S:(n + 1) * S], l1_vbd[:, (j - 1) % 2, n, :],
                                      PT[:, u % 2, n * S:(n + 1) * S], start=True, stop=True)
                        last.then_inc(pv_done, 1)
                    if j >= 2:
                        t = j - 2
                        pe.wait_ge(o_taken, L1_U + t + 1)
                        if t == 0:
                            pe.wait_ge(acc_free, 1)
                        for m in range(DT):
                            last = mm(acc[m][:, :], w_o[:, t, m * P:(m + 1) * P], l1_att[:, t % 2, :],
                                      start=(t == 0), stop=(t == JT - 1))
                        last.then_inc(wo_done, 1)
                        if t == JT - 1:
                            pass
                mean_sums(2)
                norm_sums(2, sq_ready, 6)
                norm_spread(2)
                NF = L1_FF // P
                for j in range(NF + 1):
                    if j < NF:
                        b = fill(pe, ("l1h", j))
                        for k in range(DT):
                            if j == 0:
                                pe.wait_ge(xn_ready, 2 + k + 1)
                            last = mm(b[:, :], w_1[:, k, j * P:(j + 1) * P], xn[:, k, :], start=(k == 0), stop=(k == DT - 1))
                        last.then_inc(full(("l1h", j)), 1)
                    if j >= 1:
                        t = j - 1
                        pe.wait_ge(hid_ready, t + 1)
                        if t == 0:
                            pe.wait_ge(acc_free, 2)
                        for m in range(DT):
                            last = mm(acc[m][:, :], w_2[:, t, m * P:(m + 1) * P], l1_hid[:, t % 3, :],
                                      start=(t == 0), stop=(t == NF - 1))
                        last.then_inc(w2_done, 1)

                def experts(b, rows, w_l, w_v, src_l, src_v, every, need=None):
                    for k in range(len(w_l)):
                        if need:
                            pe.wait_ge(xn_ready, need[0] + k + 1)
                        mm(b[0:rows, :], w_l[k], src_l[k], start=(k == 0), stop=(not every and k == len(w_l) - 1))
                    for k in range(len(w_v)):
                        if need:
                            pe.wait_ge(xv_ready, need[1] + k + 1)
                        if every:
                            last = mm(b[0:rows, :], w_v[k], src_v[k], start=False, stop=(k == len(w_v) - 1))
                        else:
                            last = mm(by_batch(b[0:rows, :])[:, :, LATE:S], w_v[k], by_batch(src_v[k])[:, :, LATE:S],
                                      start=False, stop=(k == len(w_v) - 1), skip_group_check=True)
                    return last

                def layer(n, every):
                    li = n - 2
                    pe.wait_ge(w_loaded[n], 16 * (4 + 3 + 8))
                    norm_sums(3 * n - 3, sq_ready, 2 * (3 * n - 3) + 2)
                    norm_spread(3 * n - 3)
                    xn_base, xv_base = 4 + 6 * li, 4 * li
                    for i in range(4):
                        b = fill(pe, ("qk", n, i))
                        at = (i // 2) * P + (D if i % 2 == 0 else 0)
                        experts(b, P, [w_qkv[n, "l"][:, k, at:at + P] for k in range(DT)],
                                [w_qkv[n, "v"][:, k, at:at + P] for k in range(DT)],
                                [xn[:, k, :] for k in range(DT)], [xv[:, k, :] for k in range(DT)], every,
                                (xn_base, xv_base) if i == 0 else None).then_inc(full(("qk", n, i)), 1)
                    for i in range(4):
                        b = fill(pe, ("rot", n, i))
                        pe.wait_ge(qk_ready, 4 * li + i + 1)
                        mm(b[:, :], rotate[:, :], qk[:, i, :], start=True, stop=True).then_inc(full(("rot", n, i)), 1)
                    for i in range(2):
                        b = fill(pe, ("v", n, i))
                        for c in range(2):
                            p = 2 * i + c
                            for k, (e, src) in enumerate((e, src) for e, src in (("l", xn), ("v", xv)) for _ in range(DT)):
                                last = mm(b[:, c * D:(c + 1) * D], src[:, k % DT, p * P:(p + 1) * P],
                                          w_qkv[n, e][:, k % DT, 2 * D:3 * D], start=(k == 0), stop=(k == 3))
                        last.then_inc(full(("v", n, i)), 1)

                    def self_scores(i):
                        u, t, p = SELF_U(n) + i, i // PAIRS, i % PAIRS
                        pe.wait_ge(shifted, u - 1)
                        pe.wait_ge(roped, 4 * li + 2 * t + 2)
                        sc = score_bank[u % 2]
                        mm(sc[:, :].rearrange("p (h s) -> p h s", h=8), ident_bf[:, :],
                           causal_bf[:, :].unsqueeze(1).broadcast_to([P, 8, S]), start=True, stop=True)
                        for r in range(2):
                            b = 2 * p + r
                            pe.wait_ge(kbd_ready[r], 12 * li + i + 1)
                            last = mm(sc[64 * r:64 * r + 64, :], qk[:, 2 * t + 1, b * S:(b + 1) * S], kbd[:, i % 2, r, :],
                                      start=False, stop=True, skip_group_check=True)
                        last.then_inc(scores_ready, 1)

                    def self_pv(i):
                        u, t, p = SELF_U(n) + i, i // PAIRS, i % PAIRS
                        pe.wait_ge(pt_ready, u + 1)
                        pe.wait_ge(o_taken, u)
                        for c in range(4):
                            for r in range(2):
                                last = mm(o_bank[32 * c:32 * c + 32, r * S:(r + 1) * S], v_self[:, 2 * p + r, 4 * t + c, :],
                                          PT[:, u % 2, c * P + r * S:c * P + (r + 1) * S], start=True, stop=True)
                        for c in range(4):
                            last = mm(o_bank[32 * c:32 * c + 32, P:2 * P], self_sum[:, :], PT[:, u % 2, c * P:(c + 1) * P], start=True, stop=True)
                        last.then_inc(pv_done, 1)

                    for i in range(8 + 3):
                        if i < 8:
                            self_scores(i)
                        if 2 <= i < 10:
                            transposes_unit(SELF_U(n) + i - 2, T)
                        if i == 3:
                            pe.wait_ge(v_ready, 2 * li + 2)
                        if i >= 3:
                            self_pv(i - 3)
                    pe.wait_ge(att_ready, 8 * (li + 1))
                    for m in range(DT):
                        b = fill(pe, ("dense", n, m))
                        experts(b, P, [w_dense[n, "l"][:, k, m * P:(m + 1) * P] for k in range(DT)],
                                [w_dense[n, "v"][:, k, m * P:(m + 1) * P] for k in range(DT)],
                                [xn[:, k, :] for k in range(DT)], [xv[:, k, :] for k in range(DT)], every
                                ).then_inc(full(("dense", n, m)), 1)
                    b = fill(pe, ("ck", n))
                    mm(b[:, :], w_ckv[n][:, 0:E], ctxT[:, :], start=True, stop=True).then_inc(full(("ck", n)), 1)
                    norm_sums(3 * n - 2, sq_ready, 2 * (3 * n - 2) + 2)
                    b = fill(pe, ("cv", n))
                    for p in range(PAIRS):
                        last = mm(b[:, p * P:(p + 1) * P], ctxT[:, p * P:(p + 1) * P], w_ckv[n][:, E:2 * E], start=True, stop=True)
                    last.then_inc(full(("cv", n)), 1)
                    norm_spread(3 * n - 2)
                    b = fill(pe, ("cq", n))
                    for k in range(DT):
                        pe.wait_ge(xn_ready, xn_base + 3 + k)
                        last = mm(b[:, :], w_cq[n][:, k, :], xn[:, k, :], start=(k == 0), stop=(k == DT - 1))
                    last.then_inc(full(("cq", n)), 1)

                    def cross_scores(i):
                        u, p, r8 = CROSS_U(n) + i, i // 2, i % 2
                        pe.wait_ge(shifted, u - 1)
                        sc = score_bank[u % 2]
                        for r in range(2):
                            b = 2 * p + r
                            pe.wait_ge(kbd_ready[r], 12 * li + 8 + p + 1)
                            last = mm(sc[64 * r:64 * r + 64, :], qk[64 * r8:64 * r8 + 64, 0, b * S:(b + 1) * S],
                                      kbd[64 * r8:64 * r8 + 64, p % 2, r, :], start=True, stop=True)
                        last.then_inc(scores_ready, 1)

                    def cross_pv(i):
                        u, p, r8 = CROSS_U(n) + i, i // 2, i % 2
                        pe.wait_ge(pt_ready, u + 1)
                        pe.wait_ge(o_taken, u)
                        pe.wait_ge(vc_ready, 4 * li + p + 1)
                        for r in range(2):
                            for c in range(4):
                                at = 64 * r8 + 32 * (c // 2)
                                last = mm(o_bank[at:at + 32, r * S:(r + 1) * S], v_cross[:, p % 2, r, 4 * r8 + c, :],
                                          PT[:, u % 2, c * P + r * S:c * P + (r + 1) * S], start=(c % 2 == 0), stop=(c % 2 == 1))
                        for c in range(4):
                            at, f = 64 * r8 + 32 * (c // 2), c % 2
                            last = mm(o_bank[at:at + 32, P:2 * P], cross_sum[:, 16 - 16 * f:48 - 16 * f], PT[:, u % 2, c * P:(c + 1) * P],
                                      start=(f == 0), stop=(f == 1))
                        last.then_inc(pv_done, 1)

                    pe.wait_ge(cq_ready, li + 1)
                    for i in range(8 + 3):
                        if i < 8:
                            cross_scores(i)
                        if 2 <= i < 10:
                            transposes_unit(CROSS_U(n) + i - 2, T)
                        if i >= 3:
                            cross_pv(i - 3)
                    pe.wait_ge(o_taken, CROSS_U(n) + 8)
                    for m in range(DT):
                        b = fill(pe, ("cdense", n, m))
                        mm(b[:, :], w_cdense[n][:, m * P:(m + 1) * P], xv[:, 0, :], start=True, stop=True
                           ).then_inc(full(("cdense", n, m)), 1)
                    norm_sums(3 * n - 1, sq_ready, 2 * (3 * n - 1) + 2)
                    norm_spread(3 * n - 1)
                    for j in range(FT + 1):
                        if j < FT:
                            rows = P if j < FT - 1 else FR
                            for key, w in (("g", w_g), ("u", w_u)):
                                b = fill(pe, (key, n, j))
                                experts(b, rows, [w[n, "l"][:, k, j * P:j * P + rows] for k in range(DT)],
                                        [w[n, "v"][:, k, j * P:j * P + rows] for k in range(DT)],
                                        [xn[:, k, :] for k in range(DT)], [xv[:, k, :] for k in range(DT)], every,
                                        (xn_base + 4, xv_base + 2) if j == 0 and key == "g" else None).then_inc(full((key, n, j)), 1)
                        if j >= 1:
                            t = j - 1
                            rows = P if t < FT - 1 else FR
                            pe.wait_ge(hl_ready, FT * li + t + 1)
                            pe.wait_ge(hv_ready, FT * li + t + 1)
                            if t == 0:
                                pe.wait_ge(acc_free, 3 + li)
                            for m in range(DT):
                                mm(acc[m][:, :], w_down[n, "l"][0:rows, t, m * P:(m + 1) * P], hid_l[t % 2][0:rows, :],
                                   start=(t == 0), stop=(not every and t == FT - 1), skip_group_check=every)
                                wv, hv = w_down[n, "v"][0:rows, t, m * P:(m + 1) * P], hid_v[0:rows, t % 2, :]
                                if every:
                                    last = mm(acc[m][:, :], wv, hv, start=False, stop=(t == FT - 1), skip_group_check=True)
                                else:
                                    last = mm(by_batch(acc[m][:, :])[:, :, LATE:S], wv, by_batch(hv)[:, :, LATE:S],
                                              start=False, stop=(t == FT - 1), skip_group_check=True)
                            last.then_inc(down_done, 1)

                pe.wait_ge(early_ready, 2)
                any_early = pe.value_load(early[0:1, 1:2].bitcast(I32))
                with pe.If(any_early > 0):
                    layer(2, True)
                    layer(3, True)
                with pe.Else():
                    layer(2, False)
                    layer(3, False)

                pe.wait_ge(res_done, 18)
                for i in range(2):
                    b = fill(pe, ("out", i))
                    for c in range(2):
                        for m in range(DT):
                            t = 2 * i + c
                            last = nc.tensor.transpose(b[:, c * D + m * P:c * D + (m + 1) * P], xT[:, m, t * P:(t + 1) * P], ident[:, :])
                    last.then_inc(full(("out", i)), 1)

            @block.scalar
            def _(act):
                A = nc.scalar.activation

                def copy(dst, src, key, ready):
                    A(dst, src, ACT.Copy).then_inc(ready, 1)

                def exp_unit(u, cols, scale):
                    act.wait_ge(shifted, u + 1)
                    A(Ebuf[:, u % 3, 0:cols], Ebuf[:, u % 3, 0:cols], ACT.Exp, scale=scale).then_inc(exped, 1)

                def pt_copy(u, cols):
                    act.wait_ge(pt_full, u + 1)
                    if u >= 2:
                        act.wait_ge(pv_done, u - 1)
                    A(PT[:, u % 2, 0:cols], pt_bank[:, 0:cols], ACT.Copy).then_inc(pt_ready, 1)

                def squares(src, ready, count):
                    for m in range(DT):
                        act.wait_ge(ready, count - DT + m + 1)
                        A(Ebuf[:, m, :], src[:, m, :], ACT.Square).then_inc(sq_ready, 1)

                def rms(n, then):
                    act.wait_ge(sums_ready, n + 1)
                    which = 1 if n in (1, 2) else 0
                    A(rms_cols, bank(("norm", n))[:, 0:PAIRS], ACT.Sqrt, scale=1.0 / D, bias=norm_consts[:, which:which + 1]).then_inc(rms_ready, 1)
                    load_table(then)

                tables = []

                def load_table(function):
                    if tables:
                        act.wait_ge(table_loaded, len(tables))
                    A(warm[:, :], ones[:, 0:1], function).then_inc(table_loaded, 1)
                    tables.append(function)

                for m in range(DT):
                    b = wait_full(act, ("in", "x", m))
                    A(xT[:, m, :], b[:, :], ACT.Copy).then_inc(xT_loaded, 1)
                    act.wait_ge(xT_loaded, m + 1)
                    act.sem_inc(free(("in", "x", m)), 1)
                b = wait_full(act, ("in", "ctx"))
                A(ctxT[:, :], b[:, :], ACT.Copy).then_inc(xT_loaded, 1)
                act.wait_ge(xT_loaded, 3)
                act.sem_inc(free(("in", "ctx")), 1)
                for m in range(DT):
                    b = wait_full(act, ("mem", m))
                    A(memT[:, m, :], b[:, :], ACT.Copy).then_inc(mem_ready, 1)
                    act.wait_ge(mem_ready, m + 1)
                    act.sem_inc(free(("mem", m)), 1)
                exp_unit(0, PAIRS * S, D ** -0.5)
                pt_copy(0, PAIRS * S)
                act.wait_ge(pv_done, 1)
                for m in range(DT):
                    A(xv[:, m, :], acc[m][:, :], ACT.Copy).then_inc(l0_ctx_ready, 1)
                act.wait_ge(l0_ctx_ready, 2)
                act.sem_inc(acc_free, 1)
                load_table(ACT.Sigmoid)
                act.sem_inc(o_taken, 1)
                for m in range(DT):
                    b = wait_full(act, ("gate", m))
                    A(xn[:, m, :], b[:, :], ACT.Sigmoid, bias=gain("L0_b_gate", m)).then_inc(gate_ready, 1)
                    act.wait_ge(gate_ready, m + 1)
                    act.sem_inc(free(("gate", m)), 1)
                squares(xT, gated, 4)
                load_table(ACT.Sqrt)
                rms(0, ACT.Sqrt)
                squares(xn, centred, 2)
                load_table(ACT.Sqrt)
                rms(1, ACT.Exp)
                act.wait_ge(kbd_zeroed, 1)
                for j in range(JT + 1):
                    if j < JT:
                        b = wait_full(act, ("l1k", j))
                        if j >= 2:
                            act.wait_ge(scores_ready, L1_U + j - 1)
                        for r in range(2):
                            last = A(l1_kbd[64 * r:64 * r + 64, j % 2, :, 64 * r:64 * r + 64], by_batch(b[64 * r:64 * r + 64, :]), ACT.Copy)
                            if r == 0:
                                continue
                        last.then_inc(l1_k_ready, 1)
                        act.wait_ge(l1_k_ready, j + 1)
                        act.sem_inc(free(("l1k", j)), 1)
                        b = wait_full(act, ("l1q", j))
                        A(l1_q[:, j % 2, :], b[:, :], ACT.Copy).then_inc(l1_q_ready, 1)
                        act.wait_ge(l1_q_ready, j + 1)
                        act.sem_inc(free(("l1q", j)), 1)
                    if j >= 1:
                        pt_copy(L1_U + j - 1, T)
                    if j < JT:
                        exp_unit(L1_U + j, T, L1_HD ** -0.5)
                squares(xn, centred, 4)
                load_table(ACT.Sqrt)
                rms(2, ACT.Gelu)
                for j in range(L1_FF // P):
                    b = wait_full(act, ("l1h", j))
                    if j >= 3:
                        act.wait_ge(w2_done, j - 2)
                    A(l1_hid[:, j % 3, :], b[:, :], ACT.Gelu).then_inc(hid_ready, 1)
                    act.wait_ge(hid_ready, j + 1)
                    act.sem_inc(free(("l1h", j)), 1)

                for n in (2, 3):
                    li = n - 2
                    squares(xT, res_done, 6 * n - 6)
                    load_table(ACT.Sqrt)
                    rms(3 * n - 3, ACT.Exp)
                    for i in range(4):
                        b = wait_full(act, ("qk", n, i))
                        A(qk[:, i, :], b[:, :], ACT.Copy).then_inc(qk_ready, 1)
                        act.wait_ge(qk_ready, 4 * li + i + 1)
                        act.sem_inc(free(("qk", n, i)), 1)
                    act.wait_ge(v_zeroed, 1)
                    for i in range(2):
                        b = wait_full(act, ("v", n, i))
                        for r in range(2):
                            for e in range(2):
                                src = b[64 * r:64 * r + 64, :].rearrange("p (c h e d) -> p c h e d", c=2, h=8, e=2)[:, :, :, e, :]
                                dst = v_self[64 * e:64 * e + 64, 4 * i + r:4 * i + r + 3:2, :, 16 * e:16 * e + 16]
                                last = A(dst, src, ACT.Copy)
                        last.then_inc(v_ready, 1)
                        act.wait_ge(v_ready, 2 * li + i + 1)
                        act.sem_inc(free(("v", n, i)), 1)
                    for i in range(8 + 2):
                        if i < 8:
                            exp_unit(SELF_U(n) + i, T, HD ** -0.5)
                        if i >= 2:
                            pt_copy(SELF_U(n) + i - 2, T)
                    b = wait_full(act, ("ck", n))
                    A(qk[:, 1, :], b[:, :], ACT.Copy).then_inc(ck_ready, 1)
                    act.wait_ge(ck_ready, li + 1)
                    act.sem_inc(free(("ck", n)), 1)
                    squares(xT, res_done, 6 * n - 4)
                    load_table(ACT.Sqrt)
                    rms(3 * n - 2, ACT.Exp)
                    b = wait_full(act, ("cv", n))
                    A(qk[:, 2, :], b[:, :], ACT.Copy).then_inc(cv_ready, 1)
                    act.wait_ge(cv_ready, li + 1)
                    act.sem_inc(free(("cv", n)), 1)
                    b = wait_full(act, ("cq", n))
                    A(qk[:, 0, :], b[:, :], ACT.Copy).then_inc(cq_ready, 1)
                    act.wait_ge(cq_ready, li + 1)
                    act.sem_inc(free(("cq", n)), 1)
                    def cross_values(p):
                        if p >= 2:
                            act.wait_ge(pv_done, CROSS_U(n) + 2 * p - 2)
                        for r in range(2):
                            for e in range(2):
                                src = qk[64 * r:64 * r + 64, 2, p * P:(p + 1) * P].rearrange("p (h f e d) -> p h f e d", h=4, f=2, e=2)[:, :, :, e, :]
                                dst = v_cross[64 * e:64 * e + 64, p % 2, r, :, :].rearrange("p (h f) c -> p h f c", f=2)
                                for f in range(2):
                                    last = A(dst[:, :, f, 16 * f + 8 * e:16 * f + 8 * e + 8], src[:, :, f, :], ACT.Copy)
                        last.then_inc(vc_ready, 1)

                    cross_values(0)
                    for i in range(8 + 2):
                        if i < 8:
                            exp_unit(CROSS_U(n) + i, T, CHD ** -0.5)
                        if i == 1:
                            cross_values(1)
                        if i >= 2:
                            pt_copy(CROSS_U(n) + i - 2, T)
                        if i in (5, 7):
                            cross_values((i - 1) // 2)
                    squares(xT, res_done, 6 * n - 2)
                    load_table(ACT.Sqrt)
                    rms(3 * n - 1, ACT.Silu)
                    for j in range(FT):
                        rows = P if j < FT - 1 else FR
                        b = wait_full(act, ("g", n, j))
                        if j >= 2:
                            act.wait_ge(hv_ready, FT * li + j - 1)
                            act.wait_ge(hl_ready, FT * li + j - 1)
                        A(silu_g[0:rows, j % 2, :], b[0:rows, :], ACT.Silu).then_inc(silu_ready, 1)
                        act.wait_ge(silu_ready, FT * li + j + 1)
                        act.sem_inc(free(("g", n, j)), 1)
                for i in range(2):
                    b = wait_full(act, ("out", i))
                    A(out_rows[:, 2 * i:2 * i + 2, :], b[:, :].rearrange("p (q d) -> p q d", d=D), ACT.Copy).then_inc(out_ready, 1)

            @block.vector
            def _(dve):
                V = nc.vector

                def groups(v, g):
                    return v.rearrange("p (g s) -> p g s", s=S)

                def shift_unit(u, g):
                    sc = groups(score_bank[u % 2][:, 0:g * S], g)
                    dve.wait_ge(scores_ready, u + 1)
                    if u >= 2:
                        dve.wait_ge(shifted, u - 1)
                    V.reduce_max(row_max[:, u % 2, 0:g], sc, AX_X).then_inc(maxed, 1)
                    dve.wait_ge(maxed, u + 1)
                    if u >= 3:
                        dve.wait_ge(pt_full, u - 2)
                    V.tensor_tensor(groups(Ebuf[:, u % 3, 0:g * S], g), sc,
                                    row_max[:, u % 2, 0:g].unsqueeze(2).broadcast_to([P, g, S]), ALU.subtract).then_inc(shifted, 1)

                def sum_unit(u, g):
                    dve.wait_ge(exped, u + 1)
                    if u >= 1:
                        dve.wait_ge(rcp_ready, u)
                    V.reduce_sum(row_sum[:, 0:g], groups(Ebuf[:, u % 3, 0:g * S], g), AX_X).then_inc(summed, 1)
                    dve.wait_ge(summed, u + 1)
                    if u >= 3:
                        dve.wait_ge(probs_ready, u - 2)
                    V.reciprocal(row_rcp[:, u % 3, 0:g], row_sum[:, 0:g]).then_inc(rcp_ready, 1)

                def residual(key, m):
                    b = wait_full(dve, key)
                    V.tensor_tensor(xT[:, m, :], b[:, :], xT[:, m, :], ALU.add).then_inc(res_done, 1)

                def times_gain(n, name, src):
                    done = 2 * [0, 1, 2, 4, 7].index(n)
                    for m in range(DT):
                        V.tensor_scalar(xn[:, m, :], src[:, m, :], gain(name, m), None, ALU.mult).then_inc(gained, 1)
                    return done

                def invert_rms(n):
                    dve.wait_ge(rms_ready, n + 1)
                    V.reciprocal(rstd, rms_cols).then_inc(rstd_ready, 1)
                    return wait_full(dve, ("norm", n))

                def plain_norm(n, name, dst, ready):
                    if n:
                        dve.wait_ge(res_done, 2 * n)
                    done = times_gain(n, name, xT)
                    b = invert_rms(n)
                    for m in range(DT):
                        dve.wait_ge(gained, done + m + 1)
                        last = V.tensor_tensor(dst[:, m, :], xn[:, m, :], b[:, :], ALU.mult).then_inc(ready, 1)
                    dve.wait_ge(ready, 2 * n + 2 if n == 0 else 6 * (n // 3) + 2)
                    dve.sem_inc(free(("norm", n)), 1)

                V.tensor_scalar(Ebuf[:, 0, :], tt_raw, 1.0, None, ALU.is_equal).then_inc(mask_step, 1)
                V.tensor_scalar(media_bias, media_raw, -NEG, NEG, ALU.mult, ALU.add).then_inc(bias_ready, 1)
                V.memset(by_batch(is_v[:, :])[:, :, S - 1:S], 0.0).then_inc(mask_step, 1)
                dve.wait_ge(mask_step, 2)
                same = by_batch(Ebuf[:, 0, :])
                V.tensor_tensor(by_batch(is_v[:, :])[:, :, 0:S - 1], same[:, :, 0:S - 1], same[:, :, 1:S], ALU.mult).then_inc(mask_step, 1)
                dve.wait_ge(mask_step, 3)
                dve.wait_ge(mask_step, 3)
                V.tensor_scalar(is_l[:, :], is_v[:, :], -1.0, 1.0, ALU.mult, ALU.add).then_inc(masks_ready, 1)
                V.tensor_reduce(early[:, 0:1], by_batch(is_v[:, :])[:, :, 0:LATE], mybir.AxisListType.XY, ALU.add).then_inc(early_ready, 1)
                dve.wait_ge(early_ready, 1)
                V.tensor_copy(early[:, 1:2].bitcast(I32), early[:, 0:1]).then_inc(early_ready, 1)
                for i in range(2):
                    b = wait_full(dve, ("memN", i))
                    V.tensor_copy(memN[:, i, :, :], b[:, :].rearrange("p (r d) -> p r d", r=2)).then_inc(memN_ready, 1)
                    dve.wait_ge(memN_ready, i + 1)
                    dve.sem_inc(free(("memN", i)), 1)
                shift_unit(0, PAIRS)
                sum_unit(0, PAIRS)
                for m in range(DT):
                    dve.wait_ge(gate_ready, m + 1)
                    V.tensor_tensor(xn[:, m, :], xn[:, m, :], xv[:, m, :], ALU.mult).then_inc(gated, 1)
                    dve.wait_ge(gated, 2 * m + 1)
                    if m == 0:
                        dve.wait_ge(gate_ready, 2)
                    V.tensor_tensor(xT[:, m, :], xT[:, m, :], xn[:, m, :], ALU.add).then_inc(gated, 1)
                dve.wait_ge(gated, 4)
                plain_norm(0, "L0_norm_w", xT, res_done)

                def layernorm(n, name):
                    b = wait_full(dve, ("mean", n))
                    for m in range(DT):
                        V.scalar_tensor_tensor(out=xn[:, m, :], in0=b[:, :], scalar=-1.0 / D, in1=xT[:, m, :],
                                               op0=ALU.mult, op1=ALU.add).then_inc(centred, 1)
                    dve.wait_ge(centred, 2 * n)
                    dve.sem_inc(free(("mean", n)), 1)
                    dve.wait_ge(sq_ready, 2 * n + 2)
                    done = times_gain(n, name + "_g", xn)
                    b = invert_rms(n)
                    for m in range(DT):
                        dve.wait_ge(gained, done + m + 1)
                        V.tensor_tensor(xn[:, m, :], xn[:, m, :], b[:, :], ALU.mult).then_inc(norm_step, 1)
                        dve.wait_ge(norm_step, 2 * (n - 1) + m + 1)
                        V.tensor_scalar(xn[:, m, :], xn[:, m, :], gain(name + "_b", m), None, ALU.add).then_inc(xn_ready, 1)
                    dve.sem_inc(free(("norm", n)), 1)

                layernorm(1, "L1_ln_q")
                dve.wait_ge(vbd_zeroed, 1)
                for j in range(JT + 1):
                    if j < JT:
                        b = wait_full(dve, ("l1v", j))
                        if j >= 2:
                            dve.wait_ge(pv_done, L1_U + j - 1)
                        for r in range(2):
                            for e in range(2):
                                src = b[64 * r:64 * r + 64, :].rearrange("p (c e d) -> p c e d", c=PAIRS, e=2)[:, :, e, :]
                                last = V.tensor_copy(l1_vbd[64 * e:64 * e + 64, j % 2, r:r + 2 * PAIRS - 1:2, 64 * e:64 * e + 64], src)
                        last.then_inc(l1_v_ready, 1)
                        dve.wait_ge(l1_v_ready, j + 1)
                        dve.sem_inc(free(("l1v", j)), 1)
                        shift_unit(L1_U + j, 8)
                    if j >= 1:
                        u, t = L1_U + j - 1, j - 1
                        dve.wait_ge(pv_done, u + 1)
                        if t >= 2:
                            dve.wait_ge(wo_done, t - 1)
                        V.tensor_copy(l1_att[:, t % 2, :], o_bank[:, :]).then_inc(o_taken, 1)
                    if j < JT:
                        sum_unit(L1_U + j, 8)

                def gated_residual(which, done, count):
                    dve.wait_ge(done, count)
                    for m in range(DT):
                        V.scalar_tensor_tensor(out=xT[:, m, :], in0=acc[m][:, :], scalar=gate_scalars[:, which:which + 1],
                                               in1=xT[:, m, :], op0=ALU.mult, op1=ALU.add).then_inc(res_done, 1)

                gated_residual(0, wo_done, JT)
                dve.wait_ge(res_done, 4)
                dve.sem_inc(acc_free, 1)
                layernorm(2, "L1_ln_ff")
                gated_residual(1, w2_done, L1_FF // P)
                dve.wait_ge(res_done, 6)
                dve.sem_inc(acc_free, 1)

                for n in (2, 3):
                    li = n - 2

                    def masked_norm(nn, name, q):
                        dve.wait_ge(res_done, 2 * nn)
                        for dst, mask in ((xn, is_l), (xv, is_v)):
                            for m in range(DT):
                                V.scalar_tensor_tensor(out=dst[:, m, :], in0=xT[:, m, :], scalar=gain(name, m), in1=mask[:, :],
                                                       op0=ALU.mult, op1=ALU.mult).then_inc(pre_step, 1)
                        b = invert_rms(nn)
                        for e, (dst, ready) in enumerate(((xn, xn_ready), (xv, xv_ready))):
                            for m in range(DT):
                                dve.wait_ge(pre_step, 4 * q + 2 * e + m + 1)
                                V.tensor_tensor(dst[:, m, :], dst[:, m, :], b[:, :], ALU.mult).then_inc(ready, 1)
                        dve.wait_ge(xv_ready, 2 * q + 2)
                        dve.sem_inc(free(("norm", nn)), 1)

                    masked_norm(3 * n - 3, f"L{n}_ln_in_w", 2 * li)

                    def rope_sin(i):
                        b = wait_full(dve, ("rot", n, i))
                        if i >= 2:
                            dve.wait_ge(roped, 4 * li + i - 1)
                        V.tensor_tensor(by_batch(PT[:, i % 2, :]), by_batch(b[:, :]),
                                        cos_sin[:, 1, :].unsqueeze(1).broadcast_to([P, G, S]), ALU.mult).then_inc(sined, 1)
                        dve.wait_ge(sined, 4 * li + i + 1)
                        dve.sem_inc(free(("rot", n, i)), 1)

                    rope_sin(0)
                    for i in range(4):
                        if i + 1 < 4:
                            rope_sin(i + 1)
                        dve.wait_ge(cosined, 4 * li + i + 1)
                        V.tensor_tensor(qk[:, i, :], qk[:, i, :], PT[:, i % 2, :], ALU.add).then_inc(roped, 1)

                    def self_keys(i):
                        u, t, p = SELF_U(n) + i, i // PAIRS, i % PAIRS
                        dve.wait_ge(roped, 4 * li + 2 * t + 1)
                        if i >= 2:
                            dve.wait_ge(scores_ready, u - 1)
                        V.tensor_tensor(*key_blocks(0, 2 * t, p, 0, i % 2), ALU.mult).then_inc(kbd_ready[0], 1)

                    def self_take(i):
                        u, t, p = SELF_U(n) + i, i // PAIRS, i % PAIRS
                        dve.wait_ge(pv_done, u + 1)
                        at = slice(p * P, (p + 1) * P)
                        V.reciprocal(xn[:, t, at], o_bank[:, P:2 * P]).then_inc(inverted, 1)
                        dve.wait_ge(inverted, 16 * li + i + 1)
                        V.tensor_tensor(xn[:, t, at], xn[:, t, at], o_bank[:, 0:P], ALU.mult).then_inc(o_taken, 1)

                    self_keys(0)
                    for i in range(8 + 3):
                        if i + 1 < 8:
                            self_keys(i + 1)
                        if i < 8:
                            shift_unit(SELF_U(n) + i, 8)
                        if i >= 3:
                            self_take(i - 3)
                    for m in range(DT):
                        residual(("dense", n, m), m)
                        dve.wait_ge(res_done, 6 * li + 6 + m + 1)
                        dve.sem_inc(free(("dense", n, m)), 1)
                    plain_norm(3 * n - 2, f"L{n}_ln_post_cross_w", xn, xn_ready)

                    def cross_keys(p):
                        if p == 0:
                            dve.wait_ge(ck_ready, li + 1)
                        if p >= 2:
                            dve.wait_ge(scores_ready, CROSS_U(n) + 2 * p - 2)
                        V.tensor_tensor(*key_blocks(1, 1, p, 0, p % 2), ALU.mult).then_inc(kbd_ready[0], 1)

                    def cross_take(i):
                        u, p, r8 = CROSS_U(n) + i, i // 2, i % 2
                        dve.wait_ge(pv_done, u + 1)
                        rows = slice(64 * r8, 64 * r8 + 64)
                        v = xv[rows, 0, p * P:(p + 1) * P]
                        V.reciprocal(v, o_bank[rows, P:2 * P]).then_inc(inverted, 1)
                        dve.wait_ge(inverted, 16 * li + 8 + i + 1)
                        V.tensor_tensor(v, v, o_bank[rows, 0:P], ALU.mult).then_inc(o_taken, 1)

                    cross_keys(0)
                    for i in range(8 + 3):
                        if i % 2 == 0 and i // 2 + 1 < PAIRS:
                            cross_keys(i // 2 + 1)
                        if i < 8:
                            shift_unit(CROSS_U(n) + i, 8)
                        if i >= 3:
                            cross_take(i - 3)
                    for m in range(DT):
                        residual(("cdense", n, m), m)
                        dve.wait_ge(res_done, 6 * li + 8 + m + 1)
                        dve.sem_inc(free(("cdense", n, m)), 1)
                    masked_norm(3 * n - 1, f"L{n}_ln_post_attn_w", 2 * li + 1)
                    for j in range(FT):
                        rows = P if j < FT - 1 else FR
                        b = wait_full(dve, ("u", n, j))
                        dve.wait_ge(silu_ready, FT * li + j + 1)
                        V.tensor_tensor(silu_g[0:rows, j % 2, :], silu_g[0:rows, j % 2, :], b[0:rows, :], ALU.mult).then_inc(h_ready, 1)
                        dve.wait_ge(h_ready, FT * li + j + 1)
                        dve.sem_inc(free(("u", n, j)), 1)
                    dve.wait_ge(down_done, FT * (li + 1))
                    for m in range(DT):
                        V.tensor_tensor(xT[:, m, :], acc[m][:, :], xT[:, m, :], ALU.add).then_inc(res_done, 1)
                    dve.wait_ge(res_done, 6 * li + 12)
                    dve.sem_inc(acc_free, 1)

            @block.gpsimd
            def _(pool):
                G_ = nc.gpsimd

                def prob_unit(u, g):
                    pool.wait_ge(rcp_ready, u + 1)
                    v = Ebuf[:, u % 3, 0:g * S].rearrange("p (g s) -> p g s", s=S)
                    G_.tensor_tensor(v, v, row_rcp[:, u % 3, 0:g].unsqueeze(2).broadcast_to([P, g, S]), ALU.mult).then_inc(probs_ready, 1)

                G_.memset(arena[:, A_K:A_K + 2048], 0.0).then_inc(kbd_zeroed, 1)
                prob_unit(0, PAIRS)
                pool.wait_ge(pv_done, 1)
                G_.memset(arena[:, A_QK:A_QK + 2048], 0.0).then_inc(vbd_zeroed, 1)
                for j in range(JT):
                    prob_unit(L1_U + j, 8)
                pool.wait_ge(wo_done, JT)
                G_.memset(arena[:, A_VS:A_VS + 3072], 0.0).then_inc(v_zeroed, 1)
                pool.wait_ge(masks_ready, 1)
                for n in (2, 3):
                    li = n - 2

                    for i in range(4):
                        pool.wait_ge(full(("rot", n, i)), PROJ["rot", n, i] // 2 + 1)
                        v = by_batch(qk[:, i, :])
                        G_.tensor_tensor(v, v, cos_sin[:, 0, :].unsqueeze(1).broadcast_to([P, G, S]), ALU.mult).then_inc(cosined, 1)
                    def self_keys(i):
                        t, p = i // PAIRS, i % PAIRS
                        pool.wait_ge(roped, 4 * li + 2 * t + 1)
                        if i >= 2:
                            pool.wait_ge(scores_ready, SELF_U(n) + i - 1)
                        G_.tensor_tensor(*key_blocks(0, 2 * t, p, 1, i % 2), ALU.mult).then_inc(kbd_ready[1], 1)

                    self_keys(0)
                    for i in range(8 + 3):
                        if i + 1 < 8:
                            self_keys(i + 1)
                        if i >= 3:
                            k = i - 3
                            t, at = k // PAIRS, slice(k % PAIRS * P, (k % PAIRS + 1) * P)
                            pool.wait_ge(o_taken, SELF_U(n) + k + 1)
                            G_.tensor_tensor(xv[:, t, at], xn[:, t, at], is_v[:, at], ALU.mult).then_inc(att_split, 1)
                            pool.wait_ge(att_split, 8 * li + k + 1)
                            G_.tensor_tensor(xn[:, t, at], xn[:, t, at], is_l[:, at], ALU.mult).then_inc(att_ready, 1)

                    def cross_keys(p):
                        if p == 0:
                            pool.wait_ge(ck_ready, li + 1)
                        if p >= 2:
                            pool.wait_ge(scores_ready, CROSS_U(n) + 2 * p - 2)
                        G_.tensor_tensor(*key_blocks(1, 1, p, 1, p % 2), ALU.mult).then_inc(kbd_ready[1], 1)

                    cross_keys(0)
                    cross_keys(1)
                    for p in range(2, PAIRS):
                        cross_keys(p)
                    for j in range(FT):
                        rows = P if j < FT - 1 else FR
                        pool.wait_ge(h_ready, FT * li + j + 1)
                        if j >= 2:
                            pool.wait_ge(down_done, FT * li + j - 1)
                        G_.tensor_tensor(hid_l[j % 2][0:rows, :], silu_g[0:rows, j % 2, :], is_l[0:rows, :], ALU.mult).then_inc(hl_ready, 1)
                        G_.tensor_tensor(hid_v[0:rows, j % 2, :], silu_g[0:rows, j % 2, :], is_v[0:rows, :], ALU.mult).then_inc(hv_ready, 1)

        nums = [s.num for s in sems]
        assert nums == list(range(nums[0], nums[0] + len(nums)))
        nc.sync.sem_clear(range(nums[0], nums[-1] + 1))
        nc.all_engine_barrier()
    ctx.close()


def kernel(**inputs):
    import concourse.bacc as _bacc
    from concourse.bass_utils import run_bass_kernel_spmd as _run

    nc = _bacc.Bacc("TRN2", target_bir_lowering=False, num_devices=1)
    rows = {"x": np.asarray(inputs["x"]).reshape(B * S, D), "ctx": np.asarray(inputs["ctx_1024"]).reshape(B * S, E),
            "types": np.asarray(inputs["mask_BxS_ik0"]).reshape(B * S), "positions": np.asarray(inputs["pos_1xS"]),
            "media_mask": np.ascontiguousarray(inputs["mask_BxS2_bk0"]).view(np.int32),
            "L0_W_memT": np.asarray(inputs["L0_xattn_W_mem"]).T, "L0_W_gateT": np.asarray(inputs["L0_xattn_W_gate"]).T}
    for name, v in inputs.items():
        if "_xattn_" in name and name not in ("L0_xattn_W_mem", "L0_xattn_W_gate"):
            rows[name.replace("_xattn_", "_")] = np.asarray(v)
    rows["c_ident"] = np.eye(P, dtype=np.float32)
    half = HD // 2
    turn = np.zeros((P, P), np.float32)
    for j in range(P):
        turn[j + half if j % HD < half else j - half, j] = -1.0 if j % HD < half else 1.0
    rows["c_rotate"] = turn
    lane = np.arange(P)
    rows["c_head_rows"] = np.stack([lane[:, None] // HD == np.arange(8), (lane[:, None] % 64) // CHD == np.arange(8)], 1).astype(np.float32)
    rows["c_self_sum"] = (np.arange(32)[None, :] // 16 == lane[:, None] // 64).astype(np.float32)
    rows["c_cross_sum"] = (np.arange(48)[None, :] // 8 == 2 + lane[:, None] // 64).astype(np.float32)
    rows["c_causal"] = np.where(np.arange(S)[None, :] <= (lane % S)[:, None], 0.0, NEG).astype(np.float32)
    inv = (1.0 / np.float32(10000.0) ** (np.arange(0, HD, 2, dtype=np.float32) / np.float32(HD))).astype(np.float32)
    angle = np.outer(np.arange(S, dtype=np.float32), inv)[:, (lane % HD) % half]
    rows["c_cos_sin"] = np.concatenate([np.cos(angle), np.sin(angle)], 1).astype(np.float32)
    rows["c_index"] = np.arange(S, dtype=np.float32)[:, None]
    rows["c_parity"] = (lane[None, :] // 64 == np.arange(2)[:, None]).astype(np.float32)
    arrays, args = {}, {}
    for name, v in rows.items():
        arrays[f"in_{name}"] = np.ascontiguousarray(v)
        args[name] = nc.dram_tensor(f"in_{name}", v.shape, mybir.dt.from_np(v.dtype), kind="ExternalInput").ap()
    out = nc.dram_tensor("out_x", (B * S, D), F32, kind="ExternalOutput").ap()
    xattn_kernel(nc, args, out)
    r = _run(nc, [arrays], core_ids=[0])
    return r.results[0]["out_x"].reshape(B, S, D)
```
